# Optimizing a Trainium2 kernel written in Bass

```python
import numpy as np
import jax
import jax.numpy as jnp

def _softmax(x, axis=-1):
    return jax.nn.softmax(x, axis=axis)

def _gelu(x):
    return jax.nn.gelu(x, approximate=True)

def _silu(x):
    return jax.nn.silu(x)

def _sigmoid(x):
    return jax.nn.sigmoid(x)

def _layernorm(x, axis=-1, eps=1e-05):
    m = jnp.mean(x, axis=axis, keepdims=True)
    v = jnp.var(x, axis=axis, keepdims=True)
    return (x - m) / jnp.sqrt(v + eps)

def _scatter_add(tgt, idx, src, axis=0):
    return tgt.at[idx].add(src)

def _segment_sum(src, seg, n):
    return jax.ops.segment_sum(src, seg, n)
kernel_name = 'mk_adaln_d1_jaxref_r8_08b360'

def setup_inputs(seed: int=0):
    np.random.seed(seed)
    _w = jnp.asarray

    def _L0_attn_setup():
        import jax, jax.numpy as jnp
        import numpy as np
        B, S, HID = (2, 256, 256)
        NH, NKV, HD = (16, 4, 128)
        KV_DIM = NKV * HD
        key = jax.random.key(seed)
        ks = jax.random.split(key, 7)
        sc = 0.02
        return {'hidden_states': jax.random.normal(ks[0], (B, S, HID), dtype=jnp.float32), 'Wq': jax.random.normal(ks[1], (NH * HD, HID), dtype=jnp.float32) * sc, 'Wk': jax.random.normal(ks[2], (KV_DIM, HID), dtype=jnp.float32) * sc, 'Wv': jax.random.normal(ks[3], (KV_DIM, HID), dtype=jnp.float32) * sc, 'Wo': jax.random.normal(ks[4], (HID, NH * HD), dtype=jnp.float32) * sc, 'bo': jnp.zeros((HID,), dtype=jnp.float32)}
    _L0_attn_in = _L0_attn_setup()

    def _L0_ffn_setup():
        import jax, jax.numpy as jnp
        import numpy as np
        HIDDEN = 256
        INTER = 688
        LUT_SIZE = 16

        def _ghost_linear(x, idx, lut):
            w = lut[idx]
            return jnp.einsum('bsh,oh->bso', x, w)
        key = jax.random.key(seed)
        k_x, k_lut, k_g, k_u, k_d = jax.random.split(key, 5)
        x = jax.random.normal(k_x, (2, 512, HIDDEN), dtype=jnp.float32)
        lut = jax.random.normal(k_lut, (LUT_SIZE,), dtype=jnp.float32) * 0.02
        gate_idx = jax.random.randint(k_g, (INTER, HIDDEN), 0, LUT_SIZE, dtype=jnp.int32)
        up_idx = jax.random.randint(k_u, (INTER, HIDDEN), 0, LUT_SIZE, dtype=jnp.int32)
        down_idx = jax.random.randint(k_d, (HIDDEN, INTER), 0, LUT_SIZE, dtype=jnp.int32)
        return {'x': x, 'lut': lut, 'gate_idx': gate_idx, 'up_idx': up_idx, 'down_idx': down_idx}
    _L0_ffn_in = _L0_ffn_setup()
    _L0_c = _w((lambda *s: np.random.randn(*s).astype(np.float32) * 0.05)(4, 256))
    _L0_wmod = _w((lambda *s: np.random.randn(*s).astype(np.float32) * 0.05)(256, 6 * 256) * 256 ** (-0.5))
    _d = {'L0_attn_hidden_states': _L0_attn_in['hidden_states'], 'L0_attn_Wq': _L0_attn_in['Wq'], 'L0_attn_Wk': _L0_attn_in['Wk'], 'L0_attn_Wv': _L0_attn_in['Wv'], 'L0_attn_Wo': _L0_attn_in['Wo'], 'L0_attn_bo': _L0_attn_in['bo'], 'L0_ffn_lut': _L0_ffn_in['lut'], 'L0_ffn_gate_idx': _L0_ffn_in['gate_idx'], 'L0_ffn_up_idx': _L0_ffn_in['up_idx'], 'L0_ffn_down_idx': _L0_ffn_in['down_idx'], 'L0_c': _L0_c, 'L0_wmod': _L0_wmod}
    _x0 = _d['L0_attn_hidden_states']
    _d['L0_attn_hidden_states'] = jax.random.normal(jax.random.fold_in(jax.random.key(seed), 1), (4, 512, 256), dtype=_x0.dtype)
    del _x0
    return _d

def reference(L0_attn_hidden_states, L0_attn_Wq, L0_attn_Wk, L0_attn_Wv, L0_attn_Wo, L0_attn_bo, L0_ffn_lut, L0_ffn_gate_idx, L0_ffn_up_idx, L0_ffn_down_idx, L0_c, L0_wmod):

    def _L0_attn_ref(hidden_states, Wq, Wk, Wv, Wo, bo):
        import jax, jax.numpy as jnp
        import numpy as np
        B, S, HID = (2, 256, 256)
        NH, NKV, HD = (16, 4, 128)
        KV_DIM = NKV * HD
        b, s, _ = hidden_states.shape
        q = (hidden_states @ Wq.T).reshape(b, s, NH, HD).transpose(0, 2, 1, 3)
        k = (hidden_states @ Wk.T).reshape(b, s, NKV, HD).transpose(0, 2, 1, 3)
        v = (hidden_states @ Wv.T).reshape(b, s, NKV, HD).transpose(0, 2, 1, 3)
        g = NH // NKV
        k_rep = jnp.repeat(k, g, axis=1)
        v_rep = jnp.repeat(v, g, axis=1)
        qf = q.astype(jnp.float32)
        kf = k_rep.astype(jnp.float32)
        scores = jnp.einsum('bhqd,bhkd->bhqk', qf, kf)
        causal = jnp.tril(jnp.ones((s, s), dtype=bool))[None, None]
        neg = jnp.finfo(scores.dtype).min
        scores = jnp.where(causal, scores, neg)
        attn = jax.nn.softmax(scores, axis=-1).astype(v.dtype)
        out = jnp.einsum('bhqk,bhkd->bhqd', attn, v_rep)
        out = out.transpose(0, 2, 1, 3).reshape(b, s, NH * HD)
        return out @ Wo.T + bo

    def _L0_ffn_ref(x, lut, gate_idx, up_idx, down_idx):
        import jax, jax.numpy as jnp
        import numpy as np
        HIDDEN = 256
        INTER = 688
        LUT_SIZE = 16

        def _ghost_linear(x, idx, lut):
            w = lut[idx]
            return jnp.einsum('bsh,oh->bso', x, w)
        gate = _ghost_linear(x, gate_idx, lut)
        up = _ghost_linear(x, up_idx, lut)
        h = jax.nn.silu(gate) * up
        return _ghost_linear(h, down_idx, lut)
    x = L0_attn_hidden_states
    mod = (_silu(L0_c) @ L0_wmod).reshape(L0_c.shape[0], 6, 1, -1)
    sa, ca, ga, sb, cb, gb = (mod[:, 0], mod[:, 1], mod[:, 2], mod[:, 3], mod[:, 4], mod[:, 5])
    ga = (2 * (ga >= 0) - 1) * jnp.maximum(jnp.abs(ga), 0.25)
    gb = (2 * (gb >= 0) - 1) * jnp.maximum(jnp.abs(gb), 0.25)
    h = _layernorm(x, axis=-1) * (1 + ca) + sa
    x = x + ga * _L0_attn_ref(h, L0_attn_Wq, L0_attn_Wk, L0_attn_Wv, L0_attn_Wo, L0_attn_bo)
    h = _layernorm(x, axis=-1) * (1 + cb) + sb
    x = x + gb * _L0_ffn_ref(h, L0_ffn_lut, L0_ffn_gate_idx, L0_ffn_up_idx, L0_ffn_down_idx)
    return x

_drawn_inputs = setup_inputs


def setup_inputs(seed=0):
    import zlib

    import numpy as np

    out = dict(_drawn_inputs(seed))
    spreads = {'L0_attn_bo': (0.0, 0.331)}
    factors = {'L0_attn_Wq': 4.878,
     'L0_attn_Wk': 4.669,
     'L0_attn_Wv': 3.856,
     'L0_attn_Wo': 3.871,
     'L0_ffn_lut': 5.442}
    for name, (base, spread) in spreads.items():
        noise = np.random.default_rng([zlib.crc32(name.encode()), seed]).standard_normal(out[name].shape)
        drawn = base * np.exp(spread * noise) if base else spread * noise
        out[name] = jnp.asarray(drawn.astype(out[name].dtype))
    for name, factor in factors.items():
        out[name] = (out[name] * factor).astype(out[name].dtype)
    return out
```

```python
from contextlib import ExitStack

import concourse.bass as bass
from concourse import mybir

F32 = mybir.dt.float32
F16 = mybir.dt.float16
I32 = mybir.dt.int32
ALU = mybir.AluOpType
ACT = mybir.ActivationFunctionType
AX = mybir.AxisListType

P = 128
NB, S, HID = 4, 512, 256
NG, NR, HD = 4, 4, 128
NT = S // P
NC = HID // P
NQ = NG * NR * HD
INTER = 688
FT = -(-INTER // P)
LAST_F = INTER - (FT - 1) * P
LUT = 16
STEPS = NG * NT
EPS = 1e-5
NEG = -3e38
SC = 64.0
GUARD = 0.25

TILE_OF = [3, 0, 2, 1]
OFF = [sum(TILE_OF[m] + 1 for m in range(r)) for r in range(NT)]
KT = sum(t + 1 for t in range(NT))
LAG_PV, LAG_O = 2, 3
PRING = 4

CHUNKS = [("k", 0), ("q", 0), ("v", 0), ("q", 1), ("o", 0), ("q", 2), ("o", 1), ("q", 3), ("o", 2), ("o", 3)]
CHUNKS_EARLY = 4
CHUNK_SLOTS = {1: [4], 2: [5], 4: [6], 5: [7], 7: [8], 8: [9]}
CH = NC * 512

HALF = INTER // 2
PIECES = ([("gate", c, h * HALF, HALF, P) for h in range(2) for c in range(NC)]
          + [("up", c, h * HALF, HALF, P) for h in range(2) for c in range(NC)]
          + [("down", f, 0, HID, P if f < FT - 1 else LAST_F) for f in range(FT)])
PIECE_SLOT0 = STEPS - len(PIECES)


LN2_SLOT = 3
LN1_SLOT = 9


def gu_items(w):
    items = [("gu", w, 0, 0)]
    for n in range(1, FT):
        items += [("gu", w, n, 0), ("hh", w, n - 1, 0)]
    return items + [("hh", w, FT - 1, 0)]


def q_items(w, g):
    return [("k", w, g, 0)] + [("q", w, g, h) for h in range(NR)]


def fillers(first, last):
    f = [[] for _ in range(STEPS)]

    def put(slots, items):
        for n, it in enumerate(items):
            f[slots[n * len(slots) // len(items)]].append(it)

    put([0, 1, 2, 3], q_items(0, 1))
    put([4, 5, 6, 7], q_items(0, 2))
    put([5, 6, 7], [("v", 0, 1, t) for t in range(NT)])
    put([8, 9, 10], q_items(0, 3))
    if first:
        put([0, 1], [("row", 0, b, 0) for b in range(NB)])
    else:
        put([4], [("h2", -1, c, 0) for c in range(NC)])
        put([5, 6, 7, 8, 9, 10], gu_items(-1))
        put([11, 12, 13], [("dn", -1, i, 0) for i in range(NT)])
    if not last:
        put([11], [("h1", 1, c, 0) for c in range(NC)])
        put([12, 13, 14], q_items(1, 0))
        put([15], [("v", 1, 0, t) for t in range(NT)])
    for s in range(STEPS):
        if not first or s >= LAG_O:
            f[s].insert(0, ("o", 0 if s >= LAG_O else -1, (s - LAG_O) % STEPS, 0))
    return f


PROLOGUE = [("h1", 0, c, 0) for c in range(NC)] + q_items(0, 0) + [("v", 0, 0, t) for t in range(NT)]


TAIL = [("h2", 0, c, 0) for c in range(NC)] + gu_items(0) + [("dn", 0, i, 0) for i in range(NT)]


def banks_of(kind):
    return {"gu": 2, "hh": 0}.get(kind, 1)


def share(items, n):
    return [it for k, it in enumerate(items) if k * NR // len(items) == n]


def key_tile(b, s, j):
    return b * (NG * KT) + (s // NT) * KT + OFF[s % NT] + j


def block_program(nc, x, wqT, wkT, wvT, woT, bo, lut, gate_iT, up_iT, down_iT, cT, wmod, out):
    with ExitStack() as ctx:
        def sb(name, shape, dt):
            return ctx.enter_context(nc.sbuf_tensor(name, shape, dt))

        def ps(name):
            return ctx.enter_context(nc.psum_tensor(name, [P, 512], F32))

        def sem(name):
            return ctx.enter_context(nc.semaphore(name))

        wq = sb("wq", [P, 2, NC, NQ], F16)
        wk = sb("wk", [P, 2, NC, NG * HD], F16)
        wv = sb("wv", [P, 2, NC, NG * HD], F16)
        wo = sb("wo", [P, 2, NG * NR, HID], F16)
        wffn = {"gate": sb("wg", [P, 2, NC, INTER], F16), "up": sb("wu", [P, 2, NC, INTER], F16),
                "down": sb("wd", [P, 2, FT, HID], F16)}
        hT = [sb("h1T", [P, 2, NC, S], F16), sb("h2T", [P, 2, NC, S], F16)]
        qT = sb("qT", [P, 2, 2, NR, S], F16)
        kT = sb("kT", [P, 2, 2, S], F16)
        vS = sb("vS", [P, 2, 2, NT, 2 * HD], F16)
        pT = sb("pT", [P, 2, 2, NR * P], F16)
        oT = sb("oT", [P, 2, 2, NR, P], F16)
        hidT = sb("hidT", [P, 2, FT, S], F16)
        prob = sb("prob", [P, PRING, NR, S], F32)
        nmax = sb("nmax", [P, PRING, NR], F32)
        rsum = sb("rsum", [P, PRING, NR], F32)
        rinv = sb("rinv", [P, PRING, NR], F32)
        xn = [sb("xn1", [P, NT, HID], F32), sb("xn2", [P, NT, HID], F32)]
        x1 = sb("x1", [P, NT, HID], F32)
        acc = sb("acc", [P, NT, HID], F32)
        outb = sb("outb", [P, 2, HID], F32)
        hf = sb("hf", [P, 2, NC, S], F32)
        act_t = sb("act_t", [P, 2, S], F32)
        stats = sb("stats", [P, 2, NT, 6], F32)
        mv = sb("mv", [P, 2, NT, 2], F32)
        rstd = sb("rstd", [P, 2, NT], F32)
        nmr = sb("nmr", [P, 2, NT], F32)
        modT = sb("modT", [P, 4, NC, NB], F32)
        grow = sb("grow", [P, NB, 2, HID], F32)
        bo_row = sb("bo_row", [P, HID], F32)
        ident = sb("ident", [P, P], F32)
        mask = sb("mask", [P, S], F32)
        mhalf = sb("mhalf", [P, NT], F32)
        stage = sb("stage", [P, 2, CH], F32)
        idx = sb("idx", [P, 2, HALF], I32)
        bits = sb("bits", [P, 3, HALF], I32)
        pick = sb("pick", [P, 4, HALF], I32)
        lutb = sb("lutb", [P, LUT], F32)
        luts = sb("luts", [P, LUT], F32)
        lutx = sb("lutx", [P, LUT // 2], I32)
        cin = sb("cin", [P, NC, NB], F32)
        cth = sb("cth", [P, NC, NB], F32)
        csl = sb("csl", [P, NC, NB], F32)
        flat = prob[:, 2:4, :, :].rearrange("p a h n -> p (a h n)")
        wm = flat[:, 0:NC * 6 * HID].rearrange("p (c n) -> p c n", c=NC)
        crep = flat[:, NC * 6 * HID:NC * 6 * HID + NC * NB * P].rearrange("p (c b n) -> p c b n", c=NC, b=NB)

        sc_ps = [ps("sc0"), ps("sc1")]
        pt_ps = [ps("pt0"), ps("pt1")]
        ot_ps = [ps("ot0"), ps("ot1")]
        gen = [ps("gen0"), ps("gen1")]

        ident_set, mask_set, half_set, ident_0, mask_0 = (sem(n) for n in
                                                          ("ident_set", "mask_set", "half_set", "ident_0", "mask_0"))
        c_in, wm_in, lut_in, bo_in = sem("c_in"), sem("wm_in"), sem("lut_in"), sem("bo_in")
        x_in, x1_in = sem("x_in"), sem("x1_in")
        stage_in = [sem("stage_in0"), sem("stage_in1")]
        idx_in = [sem("idx_in0"), sem("idx_in1")]
        out_sent = [sem("out_sent0"), sem("out_sent1")]
        c_tanh, c_twice, c_silu, c_rep, mod_mm, mod_out = (sem(n) for n in
                                                           ("c_tanh", "c_twice", "c_silu", "c_rep", "mod_mm", "mod_out"))
        row_mm, row_sgn, row_out = sem("row_mm"), sem("row_sgn"), sem("row_out")
        w_hi, w_lo = sem("w_hi"), sem("w_lo")
        lut_step, piece_w, piece_hi, piece_lo = sem("lut_step"), sem("piece_w"), sem("piece_hi"), sem("piece_lo")
        sc_mm, sc_max, sc_exp, p_rs, p_inv, p_norm = (sem(n) for n in
                                                      ("sc_mm", "sc_max", "sc_exp", "p_rs", "p_inv", "p_norm"))
        pt_mm, pt_hi, pt_lo, pv_mm = sem("pt_mm"), sem("pt_hi"), sem("pt_lo"), sem("pv_mm")
        ot_hi, ot_lo, o_mm, o_add = sem("ot_hi"), sem("ot_lo"), sem("o_mm"), sem("o_add")
        q_mm, q_hi, q_lo = sem("q_mm"), sem("q_hi"), sem("q_lo")
        k_mm, k_hi, k_lo = sem("k_mm"), sem("k_hi"), sem("k_lo")
        v_mm, v_hi, v_lo = sem("v_mm"), sem("v_hi"), sem("v_lo")
        ln_stat = [sem("ln1_stat"), sem("ln2_stat")]
        ln_mv = [sem("ln1_mv"), sem("ln2_mv")]
        ln_eps = [sem("ln1_eps"), sem("ln2_eps")]
        ln_rstd = [sem("ln1_rstd"), sem("ln2_rstd")]
        ln_nmr = [sem("ln1_nmr"), sem("ln2_nmr")]
        ln_xn = [sem("ln1_xn"), sem("ln2_xn")]
        h_mm = [sem("h1_mm"), sem("h2_mm")]
        h_f = [sem("h1_f"), sem("h2_f")]
        h_hi = [sem("h1_hi"), sem("h2_hi")]
        h_lo = [sem("h1_lo"), sem("h2_lo")]
        x1_gate, x1_sum = sem("x1_gate"), sem("x1_sum")
        gu_mm, gu_tanh, gu_gate, gu_hid, hid_hi, hid_lo = (sem(n) for n in
                                                           ("gu_mm", "gu_tanh", "gu_gate", "gu_hid", "hid_hi", "hid_lo"))
        dn_mm, dn_gate, dn_out = sem("dn_mm"), sem("dn_gate"), sem("dn_out")

        block = ctx.enter_context(nc.Block())

        def chunk_view(kind, g, part):
            if kind == "o":
                return wo[:, part, g * NR:(g + 1) * NR, :]
            return {"q": wq, "k": wk, "v": wv}[kind][:, part, :, g * 512:(g + 1) * 512]

        def chunk_stage(kind, n):
            a = NR if kind == "o" else NC
            return stage[:, n % 2, :].rearrange("p (a n) -> p a n", a=a)

        def batches(eng, slots, tail):
            slots(0, True, False)
            with eng.Fori(1, NB - 1) as b:
                slots(b, False, False)
            slots(NB - 1, False, True)
            tail()

        @block.sync
        def _(sp):
            def load_chunk(n):
                kind, g = CHUNKS[n]
                if n >= 2:
                    sp.wait_ge(w_lo, n - 1)
                dst = stage[:, n % 2, :]
                if kind == "o":
                    src = woT[g * NR * HD:(g + 1) * NR * HD, :].rearrange("(h d) n -> d h n", d=HD)
                    dst = dst.rearrange("p (h n) -> p h n", h=NR)
                else:
                    w = {"q": wqT, "k": wkT, "v": wvT}[kind]
                    src = w[:, g * 512:(g + 1) * 512].rearrange("(c p) n -> p c n", p=P)
                    dst = dst.rearrange("p (c n) -> p c n", c=NC)
                sp.dma_start(dst, src).then_inc(stage_in[n % 2], 16)

            def load_piece(n):
                kind, t, c0, cn, rows = PIECES[n]
                if n >= 2:
                    sp.wait_ge(piece_w, n - 1)
                src = {"gate": gate_iT, "up": up_iT, "down": down_iT}[kind]
                sp.dma_start(idx[0:rows, n % 2, 0:cn], src[t * P:t * P + rows, c0:c0 + cn]).then_inc(idx_in[n % 2], 16)

            def load_x(b):
                sp.dma_start(xn[0][:, :, :], x[b].rearrange("(t p) n -> p t n", p=P)).then_inc(x_in, 16)

            def store(b, i):
                sp.wait_ge(dn_out, NT * b + i + 1)
                sp.dma_start(out[b, i * P:(i + 1) * P, :], outb[:, i % 2, :]).then_inc(out_sent[i % 2], 16)

            sp.dma_start(cin[:, :, :], cT.rearrange("(c p) b -> p c b", p=P)).then_inc(c_in, 16)
            load_x(0)
            sp.dma_start(wm[:, :, :], wmod.rearrange("(c p) n -> p c n", p=P)).then_inc(wm_in, 16)
            for n in range(CHUNKS_EARLY):
                load_chunk(n)
            sp.dma_start(bo_row[:, :], bo.rearrange("(o n) -> o n", o=1).broadcast_to([P, HID])).then_inc(bo_in, 16)
            sp.dma_start(lutb[:, :], lut.rearrange("(o n) -> o n", o=1).broadcast_to([P, LUT])).then_inc(lut_in, 16)

            def slots(b, first, last):
                if not last:
                    sp.wait_ge(h_mm[0], NC * b + NC)
                    load_x(b + 1)
                if first:
                    sp.dma_start(x1[:, :, :], x[b].rearrange("(t p) n -> p t n", p=P)).then_inc(x1_in, 16)
                    for s in range(STEPS):
                        for n in CHUNK_SLOTS.get(s, []):
                            load_chunk(n)
                        if s >= PIECE_SLOT0:
                            load_piece(s - PIECE_SLOT0)
                else:
                    for i in range(NT):
                        store(b - 1, i)
                    for r in range(2):
                        sp.wait_ge(out_sent[r], 16 * NT // 2 * b)
                    sp.dma_start(x1[:, :, :], x[b].rearrange("(t p) n -> p t n", p=P)).then_inc(x1_in, 16)

            def tail():
                for i in range(NT):
                    store(NB - 1, i)
                for r in range(2):
                    sp.wait_ge(out_sent[r], 16 * NB * NT // 2)

            batches(sp, slots, tail)

        @block.tensor
        def _(pe):
            users = [None, None]
            turn = [0]

            def bank(sem_read, count):
                n = turn[0] % 2
                if users[n] is not None:
                    pe.wait_ge(*users[n])
                users[n] = (sem_read, count)
                turn[0] += 1
                return gen[n]

            def split_product(dst, pairs, done):
                last = None
                for n, (w, m) in enumerate(pairs):
                    for k, (a, c) in enumerate(((0, 0), (0, 1), (1, 0))):
                        last = pe.matmul(dst, w(a), m(c), start=(n == 0 and k == 0),
                                         stop=(n == len(pairs) - 1 and k == 2))
                last.then_inc(done, 1)

            def scores(b, s, n):
                g, i = s // NT, TILE_OF[s % NT]
                head = NR * (STEPS * b + s) + n
                pe.wait_ge(q_lo, NR * (NG * b + g) + n + 1)
                if n == 0:
                    pe.wait_ge(k_lo, NG * b + g + 1)
                if not (isinstance(b, int) and head < 2):
                    pe.wait_ge(sc_max, head - 1)
                split_product(sc_ps[n % 2][:, 0:(i + 1) * P],
                              [(lambda a: qT[:, g % 2, a, n, i * P:(i + 1) * P],
                                lambda c: kT[:, g % 2, c, 0:(i + 1) * P])], sc_mm)

            def transposes(b, s, j):
                kt = key_tile(b, s, j)
                if j == 0:
                    pe.wait_ge(p_norm, STEPS * b + s + 1)
                ring = (OFF[s % NT] + j) % 2
                if not (isinstance(b, int) and kt < 2):
                    pe.wait_ge(pt_lo, kt - 1)
                for n in range(NR):
                    t = pe.transpose(pt_ps[ring][:, n * P:(n + 1) * P],
                                     prob[:, s % PRING, n, j * P:(j + 1) * P], ident[:, :])
                t.then_inc(pt_mm, 1)

            def values(b, s, j):
                g, i = s // NT, TILE_OF[s % NT]
                step = STEPS * b + s
                pe.wait_ge(pt_lo, key_tile(b, s, j) + 1)
                pe.wait_ge(v_lo, 2 * NT * b + NT * (g // 2) + j + 1)
                if j == 0 and not (isinstance(b, int) and step < 2):
                    pe.wait_ge(ot_lo, step - 1)
                ring = (OFF[s % NT] + j) % 2
                for k, (a, c) in enumerate(((0, 0), (0, 1), (1, 0))):
                    mm = pe.matmul(ot_ps[s % 2][:, :], vS[:, g // 2, a, j, (g % 2) * HD:(g % 2 + 1) * HD],
                                   pT[:, ring, c, :], start=(j == 0 and k == 0), stop=(j == i and k == 2))
                mm.then_inc(pv_mm, 1)

            def out_projection(b, s):
                step, g = STEPS * b + s, s // NT
                pe.wait_ge(ot_lo, step + 1)
                if isinstance(b, int) and b == 0:
                    pe.wait_ge(w_lo, CHUNKS.index(("o", g)) + 1)
                split_product(bank(o_add, step + 1)[:, 0:HID],
                              [(lambda a, n=n: oT[:, s % 2, a, n, :], lambda c, n=n: wo[:, c, g * NR + n, :])
                               for n in range(NR)], o_mm)

            def filler(kind, b, u, v):
                if kind == "o":
                    out_projection(b, u)
                elif kind == "row":
                    dst = bank(row_out, u + 1)
                    if u == 0:
                        pe.wait_ge(c_rep, 1)
                    for half, col in ((0, 2 * HID), (1, 5 * HID)):
                        for c in range(NC):
                            mm = pe.matmul(dst[:, half * HID:(half + 1) * HID], crep[:, c, u, :],
                                           wm[:, c, col:col + HID], start=(c == 0), stop=(c == NC - 1))
                    mm.then_inc(row_mm, 1)
                elif kind in ("h1", "h2"):
                    which = int(kind == "h2")
                    pe.wait_ge(ln_xn[which], NT * (b + 1))
                    dst = bank(h_f[which], NC * b + u + 1)
                    for t in range(NT):
                        mm = pe.transpose(dst[:, t * P:(t + 1) * P], xn[which][:, t, u * P:(u + 1) * P], ident[:, :])
                    mm.then_inc(h_mm[which], 1)
                elif kind in ("q", "k"):
                    pe.wait_ge(h_lo[0], NC * (b + 1))
                    if kind == "q":
                        if isinstance(b, int) and b == 0:
                            pe.wait_ge(w_lo, CHUNKS.index(("q", u)) + 1)
                        w, col, lo, count, done = wq, (u * NR + v) * HD, q_lo, NR * (NG * b + u) + v + 1, q_mm
                    else:
                        if isinstance(b, int) and b == 0:
                            pe.wait_ge(w_lo, CHUNKS.index(("k", 0)) + 1)
                        w, col, lo, count, done = wk, u * HD, k_lo, NG * b + u + 1, k_mm
                    split_product(bank(lo, count)[:, :],
                                  [(lambda a, c=c: w[:, a, c, col:col + HD], lambda m, c=c: hT[0][:, m, c, :])
                                   for c in range(NC)], done)
                elif kind == "v":
                    if isinstance(b, int) and b == 0:
                        pe.wait_ge(w_lo, CHUNKS.index(("v", 0)) + 1)
                    pe.wait_ge(h_lo[0], NC * (b + 1))
                    split_product(bank(v_lo, 2 * NT * b + NT * u + v + 1)[:, 0:2 * HD],
                                  [(lambda a, c=c: hT[0][:, a, c, v * P:(v + 1) * P],
                                    lambda m, c=c: wv[:, m, c, u * 2 * HD:(u + 1) * 2 * HD])
                                   for c in range(NC)], v_mm)
                elif kind == "gu":
                    rows = P if u < FT - 1 else LAST_F
                    pe.wait_ge(h_lo[1], NC * (b + 1))
                    pe.wait_ge(piece_lo, (1 + (u * P + rows > HALF)) * NC + 2 * NC)
                    for name, read in (("gate", gu_gate), ("up", gu_hid)):
                        dst = bank(read, FT * b + u + 1)
                        w = wffn[name]
                        split_product(dst[0:rows, :],
                                      [(lambda a, c=c: w[:, a, c, u * P:u * P + rows],
                                        lambda m, c=c: hT[1][:, m, c, :]) for c in range(NC)], gu_mm)
                elif kind == "dn":
                    pe.wait_ge(hid_lo, FT * (b + 1))
                    pe.wait_ge(piece_lo, len(PIECES))
                    rows = [P if f < FT - 1 else LAST_F for f in range(FT)]
                    split_product(bank(dn_gate, NT * b + u + 1)[:, 0:HID],
                                  [(lambda a, f=f: hidT[0:rows[f], a, f, u * P:(u + 1) * P],
                                    lambda m, f=f: wffn["down"][0:rows[f], m, f, :]) for f in range(FT)], dn_mm)

            pe.wait_ge(wm_in, 16)
            pe.wait_ge(c_silu, 1)
            dst = bank(mod_out, 2)
            for m, kind in enumerate((0, 1, 3, 4)):
                for c in range(NC):
                    for k in range(NC):
                        mm = pe.matmul(dst[:, (m * NC + c) * NB:(m * NC + c + 1) * NB],
                                       wm[:, k, kind * HID + c * P:kind * HID + (c + 1) * P], csl[:, k, :],
                                       start=(k == 0), stop=(k == NC - 1))
            mm.then_inc(mod_mm, 1)
            pe.wait_ge(ident_set, 1)
            for kind, db, u, v in PROLOGUE:
                filler(kind, db, u, v)

            def behind(b, s, first):
                if s >= LAG_PV:
                    return b, s - LAG_PV
                return None if first else (b - 1, s - LAG_PV + STEPS)

            def slots(b, first, last):
                if not first:
                    odd = turn[0] % 2
                    users[odd], users[1 - odd] = (v_lo, 2 * NT * b + NT - 1), (v_lo, 2 * NT * b + NT)
                fill = fillers(first, last)
                for s in range(STEPS):
                    old = behind(b, s, first)
                    for n in range(NR):
                        scores(b, s, n)
                        if old:
                            tiles = TILE_OF[old[1] % NT] + 1
                            if n < tiles:
                                transposes(*old, n)
                            if 1 <= n <= tiles:
                                values(*old, n - 1)
                        for kind, db, u, v in share(fill[s], n):
                            filler(kind, b + db, u, v)
                    if old and tiles == NR:
                        values(*old, NR - 1)

            def tail():
                for s in range(STEPS, STEPS + LAG_PV):
                    old = s - LAG_PV
                    for j in range(TILE_OF[old % NT] + 1):
                        transposes(NB - 1, old, j)
                        if j:
                            values(NB - 1, old, j - 1)
                    values(NB - 1, old, TILE_OF[old % NT])
                    out_projection(NB - 1, s - LAG_O)
                out_projection(NB - 1, STEPS - 1)
                for kind, _, u, v in TAIL:
                    filler(kind, NB - 1, u, v)

            batches(pe, slots, tail)

        @block.scalar
        def _(act):
            def high(dst, src, ready, count, done, scale=1.0):
                act.wait_ge(ready, count)
                act.activation(dst, src, ACT.Copy, scale=scale).then_inc(done, 1)

            def split_weight(n):
                kind, g = CHUNKS[n]
                dst = chunk_view(kind, g, 0)
                act.wait_ge(stage_in[n % 2], 16 * (n // 2 + 1))
                act.activation(dst, chunk_stage(kind, n), ACT.Copy, scale=SC).then_inc(w_hi, 1)

            def piece(n):
                kind, t, c0, cn, rows = PIECES[n]
                act.wait_ge(piece_w, n + 1)
                act.activation(wffn[kind][0:rows, 0, t, c0:c0 + cn],
                               pick[0:rows, 0, 0:cn].bitcast(F32), ACT.Copy).then_inc(piece_hi, 1)

            def normalise(which, b, i):
                if i == 0:
                    act.wait_ge(ln_nmr[which], b + 1)
                src = xn[0] if which == 0 else x1
                act.activation(xn[which][:, i, :], src[:, i, :], ACT.Identity, bias=nmr[:, which, i:i + 1],
                               scale=rstd[:, which, i:i + 1]).then_inc(ln_xn[which], 1)

            def filler(kind, b, u, v, turn):
                if kind in ("h1", "h2"):
                    which = int(kind == "h2")
                    act.wait_ge(h_mm[which], NC * b + u + 1)
                    if u == 0 and which == 0:
                        act.wait_ge(mod_out, 2)
                    if which == 1:
                        act.wait_ge(row_out, NB)
                    act.activation(hf[:, which, u, :], gen[turn][:, :], ACT.Identity,
                                   bias=modT[:, 2 * which, u, bass.ds(b, 1)],
                                   scale=modT[:, 2 * which + 1, u, bass.ds(b, 1)]).then_inc(h_f[which], 1)
                    act.wait_ge(h_f[which], NC * b + u + 1)
                    act.activation(hT[which][:, 0, u, :], hf[:, which, u, :], ACT.Copy).then_inc(h_hi[which], 1)
                elif kind == "q":
                    high(qT[:, u % 2, 0, v, :], gen[turn][:, :], q_mm, NR * (NG * b + u) + v + 1, q_hi, 1 / SC)
                elif kind == "k":
                    high(kT[:, u % 2, 0, :], gen[turn][:, :], k_mm, NG * b + u + 1, k_hi, 1 / SC)
                elif kind == "v":
                    high(vS[:, u, 0, v, :], gen[turn][:, 0:2 * HD], v_mm, 2 * NT * b + NT * u + v + 1, v_hi, 1 / SC)
                elif kind == "gu":
                    rows = P if u < FT - 1 else LAST_F
                    n = FT * b + u
                    act.wait_ge(gu_mm, 2 * n + 2)
                    if u >= 2:
                        act.wait_ge(hid_lo, n - 1)
                    act.activation(act_t[0:rows, u % 2, :], gen[turn][0:rows, :], ACT.Tanh,
                                   scale=0.5 / SC).then_inc(gu_tanh, 1)
                elif kind == "hh":
                    rows = P if u < FT - 1 else LAST_F
                    high(hidT[0:rows, 0, u, :], act_t[0:rows, u % 2, :], gu_hid, FT * b + u + 1, hid_hi)

            act.wait_ge(c_in, 16)
            act.activation(cth[:, :, :], cin[:, :, :], ACT.Tanh, scale=0.5).then_inc(c_tanh, 1)
            for i in range(NT):
                normalise(0, 0, i)
            turn = [1]
            for kind, db, u, v in PROLOGUE:
                if kind == "k":
                    split_weight(0)
                elif kind == "q" and v == 0:
                    split_weight(1)
                elif kind == "v" and v == 0:
                    split_weight(2)
                    split_weight(3)
                filler(kind, db, u, v, turn[0] % 2)
                turn[0] += banks_of(kind)

            def high_probs(b, s, j):
                kt = key_tile(b, s, j)
                ring = (OFF[s % NT] + j) % 2
                if not (isinstance(b, int) and kt < 2):
                    act.wait_ge(pv_mm, kt - 1)
                high(pT[:, ring, 0, :], pt_ps[ring][:, :], pt_mm, kt + 1, pt_hi, SC)

            def exponent(b, s, n):
                head = NR * (STEPS * b + s) + n
                keys = (TILE_OF[s % NT] + 1) * P
                act.wait_ge(sc_max, head + 1)
                p = prob[:, s % PRING, n, 0:keys]
                act.activation(p, p, ACT.Exp, bias=nmax[:, s % PRING, n:n + 1], scale=-1.0,
                               accum_out=rsum[:, s % PRING, n:n + 1]).then_inc(sc_exp, 1)

            def high_out(b, s):
                step = STEPS * b + s
                if not (isinstance(b, int) and step < 2):
                    act.wait_ge(o_mm, step - 1)
                high(oT[:, s % 2, 0, :, :], ot_ps[s % 2][:, :].rearrange("p (h n) -> p h n", h=NR),
                     pv_mm, key_tile(b, s, TILE_OF[s % NT]) + 1, ot_hi, 1 / SC)

            def slots(b, first, last):
                fill = fillers(first, last)
                for s in range(STEPS):
                    old = (b, s - LAG_PV) if s >= LAG_PV else (None if first else (b - 1, s - LAG_PV + STEPS))
                    if first:
                        for n in CHUNK_SLOTS.get(s, []):
                            split_weight(n)
                    for n in range(NR):
                        if old and n <= TILE_OF[old[1] % NT]:
                            high_probs(*old, n)
                        exponent(b, s, n)
                        for kind, db, u, v in share(fill[s], n):
                            filler(kind, b + db, u, v, turn[0] % 2)
                            turn[0] += banks_of(kind)
                    if old:
                        high_out(*old)
                    if first and s >= PIECE_SLOT0:
                        piece(s - PIECE_SLOT0)
                    if s == LN2_SLOT and not first:
                        for i in range(NT):
                            normalise(1, b - 1, i)
                    if s == LN1_SLOT and not last:
                        for i in range(NT):
                            normalise(0, b + 1, i)

            def tail():
                for old in range(STEPS - LAG_PV, STEPS):
                    for j in range(TILE_OF[old % NT] + 1):
                        high_probs(NB - 1, old, j)
                    high_out(NB - 1, old)
                    turn[0] += 1
                turn[0] += 1
                for i in range(NT):
                    normalise(1, NB - 1, i)
                for kind, _, u, v in TAIL:
                    filler(kind, NB - 1, u, v, turn[0] % 2)
                    turn[0] += banks_of(kind)

            batches(act, slots, tail)

        @block.vector
        def _(dve):
            def hold():
                dve.nop(nofuse=True)

            def low(dst, src, hi, ready, count, done, scale):
                dve.wait_ge(ready, count)
                dve.scalar_tensor_tensor(out=dst, in0=src, scalar=scale, in1=hi,
                                         op0=ALU.mult, op1=ALU.subtract).then_inc(done, 1)

            def split_weight(n):
                kind, g = CHUNKS[n]
                low(chunk_view(kind, g, 1), chunk_stage(kind, n), chunk_view(kind, g, 0), w_hi, n + 1, w_lo, SC)

            lut_ops = [0]

            def chained(ins):
                lut_ops[0] += 1
                ins.then_inc(lut_step, 1)
                dve.wait_ge(lut_step, lut_ops[0])

            def piece(n):
                kind, t, c0, cn, rows = PIECES[n]
                dve.wait_ge(idx_in[n % 2], 16 * (n // 2 + 1))
                if n:
                    dve.wait_ge(piece_hi, n)
                src = idx[0:rows, n % 2, 0:cn]
                bit = [bits[0:rows, k, 0:cn] for k in range(3)]
                for k in range(3):
                    dve.tensor_scalar(bit[k], src, 2 << k, None, ALU.bitwise_and)
                chained(dve.tensor_scalar(src, src, 31, 31, ALU.logical_shift_left, ALU.arith_shift_right))

                def pair(slot, k):
                    chained(dve.tensor_scalar(pick[0:rows, slot, 0:cn], src, lutx[0:rows, k:k + 1],
                                              luts[0:rows, 2 * k:2 * k + 1].bitcast(I32),
                                              ALU.bitwise_and, ALU.bitwise_xor))

                def choose(slot, other, k):
                    chained(dve.copy_predicated(pick[0:rows, slot, 0:cn], bit[k], pick[0:rows, other, 0:cn]))

                for half in range(2):
                    top = half
                    pair(top, 4 * half)
                    pair(top + 1, 4 * half + 1)
                    choose(top, top + 1, 0)
                    pair(top + 1, 4 * half + 2)
                    pair(top + 2, 4 * half + 3)
                    choose(top + 1, top + 2, 0)
                    choose(top, top + 1, 1)
                dve.copy_predicated(pick[0:rows, 0, 0:cn], bit[2], pick[0:rows, 1, 0:cn]).then_inc(piece_w, 1)
                w = wffn[kind][0:rows, :, t, c0:c0 + cn]
                dve.wait_ge(piece_w, n + 1)
                dve.wait_ge(piece_hi, n + 1)
                dve.tensor_tensor(w[:, 1, :], pick[0:rows, 0, 0:cn].bitcast(F32), w[:, 0, :],
                                  ALU.subtract).then_inc(piece_lo, 1)

            def statistics(which, b, i):
                src = xn[0] if which == 0 else x1
                if which == 0 and i == 0:
                    dve.wait_ge(x_in, 16 * (b + 1))
                dve.bn_stats(stats[:, which, i, :], src[:, i, :]).then_inc(ln_stat[which], 1)
                dve.wait_ge(ln_stat[which], NT * b + i + 1)
                hold()
                dve.bn_aggr(mv[:, which, i, :], stats[:, which, i, :]).then_inc(ln_mv[which], 1)

            def variance(which, b):
                dve.wait_ge(ln_mv[which], NT * (b + 1))
                dve.tensor_scalar(mv[:, which, :, 1], mv[:, which, :, 1], EPS, None, ALU.add).then_inc(ln_eps[which], 1)
                dve.wait_ge(ln_rstd[which], b + 1)
                dve.scalar_tensor_tensor(out=nmr[:, which, :], in0=mv[:, which, :, 0], scalar=-1.0,
                                         in1=rstd[:, which, :], op0=ALU.mult, op1=ALU.mult).then_inc(ln_nmr[which], 1)

            def out_add(b, s, turn):
                g, i = s // NT, TILE_OF[s % NT]
                step = STEPS * b + s
                dve.wait_ge(o_mm, step + 1)
                if isinstance(b, int) and b == 0 and s == 0:
                    dve.wait_ge(bo_in, 16)
                if g:
                    dve.wait_ge(o_add, step - NT + 1)
                dve.scalar_tensor_tensor(out=acc[:, i, :], in0=gen[turn][:, 0:HID], scalar=1 / SC,
                                         in1=(acc[:, i, :] if g else bo_row[:, :]),
                                         op0=ALU.mult, op1=ALU.add).then_inc(o_add, 1)
                if g == NG - 1:
                    dve.wait_ge(o_add, step + 1)
                    dve.tensor_tensor(acc[:, i, :], acc[:, i, :], row(b, 0), ALU.mult).then_inc(x1_gate, 1)
                    dve.wait_ge(x1_gate, NT * b + s % NT + 1)
                    if s % NT == 0:
                        dve.wait_ge(x1_in, 16 * (b + 1))
                    dve.tensor_tensor(x1[:, i, :], x1[:, i, :], acc[:, i, :], ALU.add).then_inc(x1_sum, 1)
                    dve.wait_ge(x1_sum, NT * b + s % NT + 1)
                    dve.bn_stats(stats[:, 1, i, :], x1[:, i, :]).then_inc(ln_stat[1], 1)
                    dve.wait_ge(ln_stat[1], NT * b + s % NT + 1)
                    hold()
                    dve.bn_aggr(mv[:, 1, i, :], stats[:, 1, i, :]).then_inc(ln_mv[1], 1)

            def row(b, which):
                return grow[:, bass.ds(b, 1), which, :].rearrange("p o n -> p (o n)")

            def filler(kind, b, u, v, turn):
                if kind == "o":
                    out_add(b, u, turn)
                elif kind == "q":
                    low(qT[:, u % 2, 1, v, :], gen[turn][:, :], qT[:, u % 2, 0, v, :],
                        q_hi, NR * (NG * b + u) + v + 1, q_lo, 1 / SC)
                elif kind == "k":
                    low(kT[:, u % 2, 1, :], gen[turn][:, :], kT[:, u % 2, 0, :], k_hi, NG * b + u + 1, k_lo, 1 / SC)
                elif kind == "v":
                    low(vS[:, u, 1, v, :], gen[turn][:, 0:2 * HD], vS[:, u, 0, v, :],
                        v_hi, 2 * NT * b + NT * u + v + 1, v_lo, 1 / SC)
                elif kind == "row":
                    dve.wait_ge(row_mm, u + 1)
                    sgn, mag = hf[:, 1, 0, :], hf[:, 1, 1, :]
                    dve.tensor_scalar(sgn, gen[turn][:, :], 0.0, 2.0, ALU.is_ge, ALU.mult).then_inc(row_sgn, 1)
                    dve.wait_ge(row_sgn, 4 * u + 1)
                    dve.scalar_tensor_tensor(out=mag, in0=sgn, scalar=-1.0, in1=gen[turn][:, :],
                                             op0=ALU.add, op1=ALU.mult).then_inc(row_sgn, 1)
                    dve.wait_ge(row_sgn, 4 * u + 2)
                    dve.tensor_scalar(mag, mag, GUARD, None, ALU.max).then_inc(row_sgn, 1)
                    dve.wait_ge(row_sgn, 4 * u + 3)
                    dve.scalar_tensor_tensor(out=grow[:, u, :, :].rearrange("p a n -> p (a n)"), in0=sgn, scalar=-1.0,
                                             in1=mag, op0=ALU.add, op1=ALU.mult).then_inc(row_sgn, 1)
                    dve.wait_ge(row_sgn, 4 * u + 4)
                    dve.tensor_scalar(grow[:, u, 1, :], grow[:, u, 1, :], 1 / SC, None, ALU.mult).then_inc(row_out, 1)
                elif kind == "gu":
                    rows = P if u < FT - 1 else LAST_F
                    n = FT * b + u
                    t = act_t[0:rows, u % 2, :]
                    dve.wait_ge(gu_tanh, n + 1)
                    dve.scalar_tensor_tensor(out=t, in0=t, scalar=1.0, in1=gen[turn][0:rows, :],
                                             op0=ALU.add, op1=ALU.mult).then_inc(gu_gate, 1)
                    dve.wait_ge(gu_gate, n + 1)
                    dve.scalar_tensor_tensor(out=t, in0=t, scalar=0.5 / (SC * SC), in1=gen[1 - turn][0:rows, :],
                                             op0=ALU.mult, op1=ALU.mult).then_inc(gu_hid, 1)
                elif kind == "dn":
                    n = NT * b + u
                    dve.wait_ge(dn_mm, n + 1)
                    if u >= 2:
                        dve.wait_ge(out_sent[u % 2], 32 * b + 16 * (u // 2))
                    dve.tensor_tensor(outb[:, u % 2, :], gen[turn][:, 0:HID], row(b, 1), ALU.mult).then_inc(dn_gate, 1)
                    dve.wait_ge(dn_gate, n + 1)
                    dve.tensor_tensor(outb[:, u % 2, :], outb[:, u % 2, :], x1[:, u, :], ALU.add).then_inc(dn_out, 1)

            dve.wait_ge(c_tanh, 1)
            dve.scalar_tensor_tensor(out=cth[:, :, :], in0=cth[:, :, :], scalar=1.0, in1=cin[:, :, :],
                                     op0=ALU.add, op1=ALU.mult).then_inc(c_twice, 1)
            dve.wait_ge(c_twice, 1)
            dve.tensor_scalar(csl[:, :, :], cth[:, :, :], 0.5, None, ALU.mult).then_inc(c_silu, 1)
            dve.wait_ge(c_silu, 1)
            for i in range(NT):
                statistics(0, 0, i)
            variance(0, 0)
            dve.tensor_copy(crep[:, :, :, :], csl[:, :, :].unsqueeze(3).broadcast_to([P, NC, NB, P])).then_inc(c_rep, 1)
            dve.wait_ge(mod_mm, 1)
            md = gen[0][:, 0:4 * NC * NB].rearrange("p (m n) -> p m n", m=4)
            mt = modT[:, :, :, :].rearrange("p m c b -> p m (c b)")
            dve.tensor_copy(mt[:, 0:4:2, :], md[:, 0:4:2, :]).then_inc(mod_out, 1)
            dve.tensor_scalar(mt[:, 1:4:2, :], md[:, 1:4:2, :], 1.0, None, ALU.add).then_inc(mod_out, 1)
            turn = [1]
            for kind, db, u, v in PROLOGUE:
                if kind == "k":
                    split_weight(0)
                elif kind == "q" and v == 0:
                    split_weight(1)
                elif kind == "v" and v == 0:
                    split_weight(2)
                    split_weight(3)
                filler(kind, db, u, v, turn[0] % 2)
                turn[0] += banks_of(kind)

            def low_probs(b, s, j):
                ring = (OFF[s % NT] + j) % 2
                low(pT[:, ring, 1, :], pt_ps[ring][:, :], pT[:, ring, 0, :], pt_hi, key_tile(b, s, j) + 1, pt_lo, SC)

            def maximum(b, s, n, first):
                head = NR * (STEPS * b + s) + n
                keys = (TILE_OF[s % NT] + 1) * P
                dve.wait_ge(sc_mm, head + 1)
                if n == 0 and (s >= PRING or not first):
                    ob, os_ = (b, s - PRING) if s >= PRING else (b - 1, s - PRING + STEPS)
                    dve.wait_ge(pt_mm, key_tile(ob, os_, TILE_OF[os_ % NT]) + 1)
                if first and s == 0 and n == 0:
                    dve.wait_ge(mask_set, 1)
                if first and s == 2 and n == 0:
                    dve.wait_ge(row_mm, NB)
                hold()
                dve.tensor_tensor_reduce(out=prob[:, s % PRING, n, 0:keys], in0=sc_ps[n % 2][:, 0:keys],
                                         in1=mask[:, S - keys:S], scale=-1.0, scalar=-NEG, op0=ALU.add, op1=ALU.min,
                                         accum_out=nmax[:, s % PRING, n:n + 1]).then_inc(sc_max, 1)

            def inverse(b, s):
                step = STEPS * b + s
                dve.wait_ge(sc_exp, NR * (step + 1))
                if not (isinstance(b, int) and step < PRING):
                    dve.wait_ge(p_norm, step - PRING + 1)
                dve.reciprocal(rinv[:, s % PRING, :], rsum[:, s % PRING, :]).then_inc(p_inv, 1)

            def low_out(b, s):
                low(oT[:, s % 2, 1, :, :], ot_ps[s % 2][:, :].rearrange("p (h n) -> p h n", h=NR), oT[:, s % 2, 0, :, :],
                    ot_hi, STEPS * b + s + 1, ot_lo, 1 / SC)

            def slots(b, first, last):
                fill = fillers(first, last)
                for s in range(STEPS):
                    old = (b, s - LAG_PV) if s >= LAG_PV else (None if first else (b - 1, s - LAG_PV + STEPS))
                    if first:
                        for n in CHUNK_SLOTS.get(s, []):
                            split_weight(n)
                    for n in range(NR):
                        maximum(b, s, n, first)
                        if old and n <= TILE_OF[old[1] % NT]:
                            low_probs(*old, n)
                        for kind, db, u, v in share(fill[s], n):
                            filler(kind, b + db, u, v, turn[0] % 2)
                            turn[0] += banks_of(kind)
                    inverse(b, s)
                    if old:
                        low_out(*old)
                    if first and s == 0:
                        dve.wait_ge(lut_in, 16)
                        chained(dve.tensor_scalar(luts[:, :], lutb[:, :], SC, None, ALU.mult))
                        li = luts[:, :].bitcast(I32).rearrange("p (k two) -> p k two", two=2)
                        chained(dve.tensor_tensor(lutx[:, :], li[:, :, 0], li[:, :, 1], ALU.bitwise_xor))
                    if first and s >= PIECE_SLOT0:
                        piece(s - PIECE_SLOT0)
                    if s == LN2_SLOT and not first:
                        variance(1, b - 1)
                    if LN1_SLOT - NT <= s < LN1_SLOT and not last:
                        statistics(0, b + 1, s - LN1_SLOT + NT)
                    if s == LN1_SLOT and not last:
                        variance(0, b + 1)

            def tail():
                for old in range(STEPS - LAG_PV, STEPS):
                    for j in range(TILE_OF[old % NT] + 1):
                        low_probs(NB - 1, old, j)
                    low_out(NB - 1, old)
                    out_add(NB - 1, old - 1, turn[0] % 2)
                    turn[0] += 1
                out_add(NB - 1, STEPS - 1, turn[0] % 2)
                turn[0] += 1
                variance(1, NB - 1)
                for kind, _, u, v in TAIL:
                    filler(kind, NB - 1, u, v, turn[0] % 2)
                    turn[0] += banks_of(kind)

            batches(dve, slots, tail)

        @block.gpsimd
        def _(pool):
            pool.memset(ident[:, :], 0.0).then_inc(ident_0, 1)
            pool.wait_ge(ident_0, 1)
            pool.affine_select(out=ident[:, :], in_=ident[:, :], compare_op=ALU.not_equal, fill=1.0, base=0,
                               pattern=[[-1, P]], channel_multiplier=1).then_inc(ident_set, 1)
            pool.memset(mhalf[:, :], -0.5).then_inc(half_set, 1)
            pool.wait_ge(half_set, 1)

            def root(which, b):
                pool.wait_ge(ln_eps[which], b + 1)
                if not (isinstance(b, int) and b == 0):
                    pool.wait_ge(ln_xn[which], NT * b)
                pool.tensor_tensor(rstd[:, which, :], mv[:, which, :, 1], mhalf[:, :], ALU.pow).then_inc(ln_rstd[which], 1)

            def filler(kind, b, u, v):
                if kind in ("h1", "h2"):
                    which = int(kind == "h2")
                    pool.wait_ge(h_hi[which], NC * b + u + 1)
                    pool.tensor_tensor(hT[which][:, 1, u, :], hf[:, which, u, :], hT[which][:, 0, u, :],
                                       ALU.subtract).then_inc(h_lo[which], 1)
                elif kind == "hh":
                    rows = P if u < FT - 1 else LAST_F
                    pool.wait_ge(hid_hi, FT * b + u + 1)
                    pool.tensor_tensor(hidT[0:rows, 1, u, :], act_t[0:rows, u % 2, :], hidT[0:rows, 0, u, :],
                                       ALU.subtract).then_inc(hid_lo, 1)

            def divide(b, s):
                keys = (TILE_OF[s % NT] + 1) * P
                pool.wait_ge(p_inv, STEPS * b + s + 1)
                p = prob[:, s % PRING, :, 0:keys]
                pool.tensor_tensor(p, p, rinv[:, s % PRING, :].unsqueeze(2).broadcast_to([P, NR, keys]),
                                   ALU.mult).then_inc(p_norm, 1)

            root(0, 0)
            pool.memset(mask[:, :], 0.0).then_inc(mask_0, 1)
            pool.wait_ge(mask_0, 1)
            pool.affine_select(out=mask[:, S - P:S], in_=mask[:, S - P:S], compare_op=ALU.is_ge, fill=NEG, base=0,
                               pattern=[[-1, P]], channel_multiplier=1).then_inc(mask_set, 1)
            for kind, db, u, v in PROLOGUE:
                filler(kind, db, u, v)

            def slots(b, first, last):
                fill = fillers(first, last)
                for s in range(STEPS):
                    for n in range(NR):
                        for kind, db, u, v in share(fill[s], n):
                            filler(kind, b + db, u, v)
                    divide(b, s)
                    if s == LN2_SLOT and not first:
                        root(1, b - 1)
                    if s == LN1_SLOT and not last:
                        root(0, b + 1)

            def tail():
                root(1, NB - 1)
                for kind, _, u, v in TAIL:
                    filler(kind, NB - 1, u, v)

            batches(pool, slots, tail)


_INS = [("x", "L0_attn_hidden_states"), ("wqT", "L0_attn_Wq"), ("wkT", "L0_attn_Wk"), ("wvT", "L0_attn_Wv"),
        ("woT", "L0_attn_Wo"), ("bo", "L0_attn_bo"), ("lut", "L0_ffn_lut"), ("gate_iT", "L0_ffn_gate_idx"),
        ("up_iT", "L0_ffn_up_idx"), ("down_iT", "L0_ffn_down_idx"), ("cT", "L0_c"), ("wmod", "L0_wmod")]


def kernel(**inputs):
    import numpy as np
    import concourse.bacc as bacc
    from concourse.bass_utils import run_bass_kernel_spmd as run

    nc = bacc.Bacc("TRN2", target_bir_lowering=False, num_devices=1)
    arrays, args = {}, []
    for short, name in _INS:
        a = np.asarray(inputs[name])
        a = np.ascontiguousarray(a.T if short.endswith("T") else a)
        arrays[short] = a
        args.append(nc.dram_tensor(short, a.shape, mybir.dt.from_np(a.dtype), kind="ExternalInput").ap())
    args.append(nc.dram_tensor("y", (NB, S, HID), F32, kind="ExternalOutput").ap())
    block_program(nc, *args)
    return run(nc, [arrays], core_ids=[0]).results[0]["y"]
```

```python
from contextlib import ExitStack

import concourse.bass as bass
from concourse import mybir

F32 = mybir.dt.float32
F16 = mybir.dt.float16
I32 = mybir.dt.int32
ALU = mybir.AluOpType
ACT = mybir.ActivationFunctionType
AX = mybir.AxisListType

P = 128
NB, S, HID = 4, 512, 256
NG, NR, HD = 4, 4, 128
NT = S // P
NC = HID // P
NQ = NG * NR * HD
INTER = 688
FT = -(-INTER // P)
LAST_F = INTER - (FT - 1) * P
LUT = 16
STEPS = NG * NT
EPS = 1e-5
NEG = -3e38
SC = 64.0
GUARD = 0.25

TILE_OF = [3, 0, 2, 1]
OFF = [sum(TILE_OF[m] + 1 for m in range(r)) for r in range(NT)]
KT = sum(t + 1 for t in range(NT))
LAG_PV, LAG_O = 2, 3
PRING = 4
PTRING = 4
RING = 4

CHUNKS = [("k", 0), ("q", 0), ("v", 0), ("q", 1), ("o", 0), ("q", 2), ("o", 1), ("q", 3), ("o", 2), ("o", 3)]
CHUNKS_EARLY = 4
CHUNK_SLOTS = {1: [4], 2: [5], 4: [6], 5: [7], 7: [8], 8: [9]}
CH = NC * 512

HALF = INTER // 2
PIECES = ([("gate", c, h * HALF, HALF, P) for h in range(2) for c in range(NC)]
          + [("up", c, h * HALF, HALF, P) for h in range(2) for c in range(NC)]
          + [("down", f, 0, HID, P if f < FT - 1 else LAST_F) for f in range(FT)])
PIECE_SLOT0 = STEPS - len(PIECES)


LN2_SLOT = 3
LN1_SLOT = 9


def gu_items(w):
    items = [("gu", w, 0, 0)]
    for n in range(1, FT):
        items += [("gu", w, n, 0), ("hh", w, n - 1, 0)]
    return items + [("hh", w, FT - 1, 0)]


def q_items(w, g):
    return [("k", w, g, 0)] + [("q", w, g, h) for h in range(NR)]


def fillers(first, last):
    f = [[] for _ in range(STEPS)]

    def put(slots, items):
        for n, it in enumerate(items):
            f[slots[n * len(slots) // len(items)]].append(it)

    put([0, 1, 2, 3], q_items(0, 1))
    put([4, 5, 6, 7], q_items(0, 2))
    put([5, 6, 7], [("v", 0, 1, t) for t in range(NT)])
    put([8, 9, 10], q_items(0, 3))
    if first:
        put([0, 1], [("row", 0, b, 0) for b in range(NB)])
    else:
        put([5], [("h2", -1, c, 0) for c in range(NC)])
        put([6, 7, 8, 9, 10], gu_items(-1))
        put([11, 12, 13], [("dn", -1, i, 0) for i in range(NT)])
    if not last:
        put([11], [("h1", 1, c, 0) for c in range(NC)])
        put([12, 13, 14], q_items(1, 0))
        put([15], [("v", 1, 0, t) for t in range(NT)])
    for s in range(STEPS):
        if not first or s >= LAG_O:
            f[s].append(("o", 0 if s >= LAG_O else -1, (s - LAG_O) % STEPS, 0))
    return f


PROLOGUE = [("h1", 0, c, 0) for c in range(NC)] + q_items(0, 0) + [("v", 0, 0, t) for t in range(NT)]


TAIL = [("h2", 0, c, 0) for c in range(NC)] + gu_items(0) + [("dn", 0, i, 0) for i in range(NT)]


def banks_of(kind):
    return {"gu": 2, "hh": 0}.get(kind, 1)


def share(items, n):
    return [it for k, it in enumerate(items) if -(-(k + 1) * NR // len(items)) - 1 == n]


def back(b, s, k, first):
    if s - k >= STEPS or (first and s < k):
        return None
    return (b, s - k) if s >= k else (b - 1, s - k + STEPS)


def to_transpose(b, s, n, first):
    old = back(b, s, LAG_PV, first)
    return (*old, n) if old and n <= TILE_OF[old[1] % NT] else None


def to_multiply(b, s, n, first):
    return to_transpose(b, s, n - 2, first) if n >= 2 else to_transpose(b, s - 1, n + 2, first) if s else (
        None if first else to_transpose(b - 1, STEPS - 1, n + 2, False))


def to_collect(b, s, n, first):
    for k, at in ((LAG_PV, n), (LAG_PV + 1, n + NR)):
        old = back(b, s, k, first)
        if old and at == TILE_OF[old[1] % NT] + 3:
            return old
    return None


def in_batch(s, j):
    return (s // NT) * KT + OFF[s % NT] + j


def key_tile(b, s, j):
    return b * (NG * KT) + in_batch(s, j)


def block_program(nc, x, wqT, wkT, wvT, woT, bo, lut, gate_iT, up_iT, down_iT, cT, wmod, out):
    with ExitStack() as ctx:
        def sb(name, shape, dt):
            return ctx.enter_context(nc.sbuf_tensor(name, shape, dt))

        def ps(name):
            return ctx.enter_context(nc.psum_tensor(name, [P, 512], F32))

        def sem(name):
            return ctx.enter_context(nc.semaphore(name))

        wq = sb("wq", [P, 2, NC, NQ], F16)
        wk = sb("wk", [P, 2, NC, NG * HD], F16)
        wv = sb("wv", [P, 2, NC, NG * HD], F16)
        wo = sb("wo", [P, 2, NG * NR, HID], F16)
        wffn = {"gate": sb("wg", [P, 2, NC, INTER], F16), "up": sb("wu", [P, 2, NC, INTER], F16),
                "down": sb("wd", [P, 2, FT, HID], F16)}
        hT = [sb("h1T", [P, 2, NC, S], F16), sb("h2T", [P, 2, NC, S], F16)]
        qT = sb("qT", [P, 2, 2, NR, S], F16)
        kT = sb("kT", [P, 2, 2, S], F16)
        vS = sb("vS", [P, 2, 2, NT, 2 * HD], F16)
        pT = sb("pT", [P, PTRING, 2, NR * P], F16)
        oT = sb("oT", [P, 2, 2, NR, P], F16)
        hidT = sb("hidT", [P, 2, FT, S], F16)
        prob = sb("prob", [P, PRING, NR, S], F32)
        nmax = sb("nmax", [P, PRING, NR], F32)
        rsum = sb("rsum", [P, PRING, NR], F32)
        rinv = sb("rinv", [P, PRING, NR], F32)
        xn = [sb("xn1", [P, NT, HID], F32), sb("xn2", [P, NT, HID], F32)]
        x1 = sb("x1", [P, NT, HID], F32)
        acc = sb("acc", [P, NT, HID], F32)
        outb = sb("outb", [P, 2, HID], F32)
        hf = sb("hf", [P, 2, NC, S], F32)
        act_t = sb("act_t", [P, 2, S], F32)
        stats = sb("stats", [P, 2, NT, 6], F32)
        mv = sb("mv", [P, 2, NT, 2], F32)
        rstd = sb("rstd", [P, 2, NT], F32)
        nmr = sb("nmr", [P, 2, NT], F32)
        modT = sb("modT", [P, 4, NC, NB], F32)
        grow = sb("grow", [P, NB, 2, HID], F32)
        bo_row = sb("bo_row", [P, HID], F32)
        ident = sb("ident", [P, P], F32)
        mask = sb("mask", [P, S], F32)
        mhalf = sb("mhalf", [P, NT], F32)
        stage = sb("stage", [P, 2, CH], F32)
        idx = sb("idx", [P, 2, HALF], I32)
        spare = hidT[:, :, :, :].rearrange("p a f s -> p (a f s)").bitcast(I32)
        bits = spare[:, 0:3 * HALF].rearrange("p (k n) -> p k n", k=3)
        pick = spare[:, 3 * HALF:7 * HALF].rearrange("p (k n) -> p k n", k=4)
        lutb = sb("lutb", [P, LUT], F32)
        luts = sb("luts", [P, LUT], F32)
        lutx = sb("lutx", [P, LUT // 2], I32)
        cin = sb("cin", [P, NC, NB], F32)
        cth = sb("cth", [P, NC, NB], F32)
        csl = sb("csl", [P, NC, NB], F32)
        flat = prob[:, 2:4, :, :].rearrange("p a h n -> p (a h n)")
        wm = flat[:, 0:NC * 6 * HID].rearrange("p (c n) -> p c n", c=NC)
        crep = flat[:, NC * 6 * HID:NC * 6 * HID + NC * NB * P].rearrange("p (c b n) -> p c b n", c=NC, b=NB)

        pt_ps = [ps("pt0"), ps("pt1")]
        ot_ps = [ps("ot0"), ps("ot1")]
        gen = [ps(f"gen{n}") for n in range(RING)]

        ident_set, mask_set, half_set, ident_0, mask_0 = (sem(n) for n in
                                                          ("ident_set", "mask_set", "half_set", "ident_0", "mask_0"))
        c_in, wm_in, lut_in, bo_in = sem("c_in"), sem("wm_in"), sem("lut_in"), sem("bo_in")
        x_in, x1_in = sem("x_in"), sem("x1_in")
        stage_in = [sem("stage_in0"), sem("stage_in1")]
        idx_in = [sem("idx_in0"), sem("idx_in1")]
        out_sent = [sem("out_sent0"), sem("out_sent1")]
        c_tanh, c_twice, c_silu, c_rep, mod_mm, mod_out = (sem(n) for n in
                                                           ("c_tanh", "c_twice", "c_silu", "c_rep", "mod_mm", "mod_out"))
        row_mm, row_sgn, row_out = sem("row_mm"), sem("row_sgn"), sem("row_out")
        w_hi, w_lo = sem("w_hi"), sem("w_lo")
        lut_step, piece_w, piece_hi, piece_lo = sem("lut_step"), sem("piece_w"), sem("piece_hi"), sem("piece_lo")
        sc_mm, sc_max, sc_exp, p_rs, p_inv, p_norm = (sem(n) for n in
                                                      ("sc_mm", "sc_max", "sc_exp", "p_rs", "p_inv", "p_norm"))
        pt_mm, pt_hi, pt_lo, pv_mm = sem("pt_mm"), sem("pt_hi"), sem("pt_lo"), sem("pv_mm")
        ot_hi, ot_lo, o_mm, o_add = sem("ot_hi"), sem("ot_lo"), sem("o_mm"), sem("o_add")
        q_mm, q_hi, q_lo = sem("q_mm"), sem("q_hi"), sem("q_lo")
        k_mm, k_hi, k_lo = sem("k_mm"), sem("k_hi"), sem("k_lo")
        v_mm, v_hi, v_lo = sem("v_mm"), sem("v_hi"), sem("v_lo")
        ln_stat = [sem("ln1_stat"), sem("ln2_stat")]
        ln_mv = [sem("ln1_mv"), sem("ln2_mv")]
        ln_eps = [sem("ln1_eps"), sem("ln2_eps")]
        ln_rstd = [sem("ln1_rstd"), sem("ln2_rstd")]
        ln_nmr = [sem("ln1_nmr"), sem("ln2_nmr")]
        ln_xn = [sem("ln1_xn"), sem("ln2_xn")]
        h_mm = [sem("h1_mm"), sem("h2_mm")]
        h_f = [sem("h1_f"), sem("h2_f")]
        h_hi = [sem("h1_hi"), sem("h2_hi")]
        h_lo = [sem("h1_lo"), sem("h2_lo")]
        x1_gate, x1_sum = sem("x1_gate"), sem("x1_sum")
        gu_mm, gu_tanh, gu_gate, gu_hid, hid_hi, hid_lo = (sem(n) for n in
                                                           ("gu_mm", "gu_tanh", "gu_gate", "gu_hid", "hid_hi", "hid_lo"))
        dn_mm, dn_gate, dn_out = sem("dn_mm"), sem("dn_gate"), sem("dn_out")

        block = ctx.enter_context(nc.Block())

        def chunk_view(kind, g, part):
            if kind == "o":
                return wo[:, part, g * NR:(g + 1) * NR, :]
            return {"q": wq, "k": wk, "v": wv}[kind][:, part, :, g * 512:(g + 1) * 512]

        def chunk_stage(kind, n):
            a = NR if kind == "o" else NC
            return stage[:, n % 2, :].rearrange("p (a n) -> p a n", a=a)

        def batches(eng, slots, tail):
            slots(0, True, False)
            with eng.Fori(1, NB - 1) as b:
                slots(b, False, False)
            slots(NB - 1, False, True)
            tail()

        @block.sync
        def _(sp):
            def load_chunk(n):
                kind, g = CHUNKS[n]
                if n >= 2:
                    sp.wait_ge(w_lo, n - 1)
                dst = stage[:, n % 2, :]
                if kind == "o":
                    src = woT[g * NR * HD:(g + 1) * NR * HD, :].rearrange("(h d) n -> d h n", d=HD)
                    dst = dst.rearrange("p (h n) -> p h n", h=NR)
                else:
                    w = {"q": wqT, "k": wkT, "v": wvT}[kind]
                    src = w[:, g * 512:(g + 1) * 512].rearrange("(c p) n -> p c n", p=P)
                    dst = dst.rearrange("p (c n) -> p c n", c=NC)
                sp.dma_start(dst, src).then_inc(stage_in[n % 2], 16)

            def load_piece(n):
                kind, t, c0, cn, rows = PIECES[n]
                if n >= 2:
                    sp.wait_ge(piece_w, n - 1)
                src = {"gate": gate_iT, "up": up_iT, "down": down_iT}[kind]
                sp.dma_start(idx[0:rows, n % 2, 0:cn], src[t * P:t * P + rows, c0:c0 + cn]).then_inc(idx_in[n % 2], 16)

            def load_x(b):
                sp.dma_start(xn[0][:, :, :], x[b].rearrange("(t p) n -> p t n", p=P)).then_inc(x_in, 16)

            def store(b, i):
                sp.wait_ge(dn_out, NT * b + i + 1)
                sp.dma_start(out[b, i * P:(i + 1) * P, :], outb[:, i % 2, :]).then_inc(out_sent[i % 2], 16)

            sp.dma_start(cin[:, :, :], cT.rearrange("(c p) b -> p c b", p=P)).then_inc(c_in, 16)
            load_x(0)
            sp.dma_start(wm[:, :, :], wmod.rearrange("(c p) n -> p c n", p=P)).then_inc(wm_in, 16)
            for n in range(CHUNKS_EARLY):
                load_chunk(n)
            sp.dma_start(bo_row[:, :], bo.rearrange("(o n) -> o n", o=1).broadcast_to([P, HID])).then_inc(bo_in, 16)
            sp.dma_start(lutb[:, :], lut.rearrange("(o n) -> o n", o=1).broadcast_to([P, LUT])).then_inc(lut_in, 16)

            def slots(b, first, last):
                if not last:
                    sp.wait_ge(h_mm[0], NC * b + NC)
                    load_x(b + 1)
                if first:
                    sp.dma_start(x1[:, :, :], x[b].rearrange("(t p) n -> p t n", p=P)).then_inc(x1_in, 16)
                    for s in range(STEPS):
                        for n in CHUNK_SLOTS.get(s, []):
                            load_chunk(n)
                        if s >= PIECE_SLOT0:
                            load_piece(s - PIECE_SLOT0)
                else:
                    for i in range(NT):
                        store(b - 1, i)
                    for r in range(2):
                        sp.wait_ge(out_sent[r], 16 * NT // 2 * b)
                    sp.dma_start(x1[:, :, :], x[b].rearrange("(t p) n -> p t n", p=P)).then_inc(x1_in, 16)

            def tail():
                for i in range(NT):
                    store(NB - 1, i)
                for r in range(2):
                    sp.wait_ge(out_sent[r], 16 * NB * NT // 2)

            batches(sp, slots, tail)

        @block.tensor
        def _(pe):
            users = [None] * RING
            entry = []
            turn = [0]

            def bank(sem_read, count):
                n = turn[0] % RING
                if users[n] is not None:
                    pe.wait_ge(*users[n])
                users[n] = (sem_read, count)
                turn[0] += 1
                return gen[n]

            def split_product(dst, pairs, done):
                last = None
                for n, (w, m) in enumerate(pairs):
                    for k, (a, c) in enumerate(((0, 0), (0, 1), (1, 0))):
                        last = pe.matmul(dst, w(a), m(c), start=(n == 0 and k == 0),
                                         stop=(n == len(pairs) - 1 and k == 2))
                last.then_inc(done, 1)

            def scores(b, s, n):
                g, i = s // NT, TILE_OF[s % NT]
                head = NR * (STEPS * b + s) + n
                pe.wait_ge(q_lo, NR * (NG * b + g) + n + 1)
                if n == 0:
                    pe.wait_ge(k_lo, NG * b + g + 1)
                split_product(bank(sc_max, head + 1)[:, 0:(i + 1) * P],
                              [(lambda a: qT[:, g % 2, a, n, i * P:(i + 1) * P],
                                lambda c: kT[:, g % 2, c, 0:(i + 1) * P])], sc_mm)

            def transposes(b, s, j):
                kt = key_tile(b, s, j)
                if j == 0:
                    pe.wait_ge(p_norm, STEPS * b + s + 1)
                ring = in_batch(s, j) % 2
                if not (isinstance(b, int) and kt < 2):
                    pe.wait_ge(pt_lo, kt - 1)
                for n in range(NR):
                    t = pe.transpose(pt_ps[ring][:, n * P:(n + 1) * P],
                                     prob[:, s % PRING, n, j * P:(j + 1) * P], ident[:, :])
                t.then_inc(pt_mm, 1)

            def values(b, s, j):
                g, i = s // NT, TILE_OF[s % NT]
                step = STEPS * b + s
                pe.wait_ge(pt_lo, key_tile(b, s, j) + 1)
                pe.wait_ge(v_lo, 2 * NT * b + NT * (g // 2) + j + 1)
                if j == 0 and not (isinstance(b, int) and step < 2):
                    pe.wait_ge(ot_lo, step - 1)
                ring = in_batch(s, j) % PTRING
                for k, (a, c) in enumerate(((0, 0), (0, 1), (1, 0))):
                    mm = pe.matmul(ot_ps[s % 2][:, :], vS[:, g // 2, a, j, (g % 2) * HD:(g % 2 + 1) * HD],
                                   pT[:, ring, c, :], start=(j == 0 and k == 0), stop=(j == i and k == 2))
                mm.then_inc(pv_mm, 1)

            def out_projection(b, s):
                step, g = STEPS * b + s, s // NT
                pe.wait_ge(ot_lo, step + 1)
                if isinstance(b, int) and b == 0:
                    pe.wait_ge(w_lo, CHUNKS.index(("o", g)) + 1)
                split_product(bank(o_add, step + 1)[:, 0:HID],
                              [(lambda a, n=n: oT[:, s % 2, a, n, :], lambda c, n=n: wo[:, c, g * NR + n, :])
                               for n in range(NR)], o_mm)

            def filler(kind, b, u, v):
                if kind == "o":
                    out_projection(b, u)
                elif kind == "row":
                    dst = bank(row_out, u + 1)
                    if u == 0:
                        pe.wait_ge(c_rep, 1)
                    for half, col in ((0, 2 * HID), (1, 5 * HID)):
                        for c in range(NC):
                            mm = pe.matmul(dst[:, half * HID:(half + 1) * HID], crep[:, c, u, :],
                                           wm[:, c, col:col + HID], start=(c == 0), stop=(c == NC - 1))
                    mm.then_inc(row_mm, 1)
                elif kind in ("h1", "h2"):
                    which = int(kind == "h2")
                    pe.wait_ge(ln_xn[which], NT * (b + 1))
                    dst = bank(h_f[which], NC * b + u + 1)
                    for t in range(NT):
                        mm = pe.transpose(dst[:, t * P:(t + 1) * P], xn[which][:, t, u * P:(u + 1) * P], ident[:, :])
                    mm.then_inc(h_mm[which], 1)
                elif kind in ("q", "k"):
                    pe.wait_ge(h_lo[0], NC * (b + 1))
                    if kind == "q":
                        if isinstance(b, int) and b == 0:
                            pe.wait_ge(w_lo, CHUNKS.index(("q", u)) + 1)
                        w, col, lo, count, done = wq, (u * NR + v) * HD, q_lo, NR * (NG * b + u) + v + 1, q_mm
                    else:
                        if isinstance(b, int) and b == 0:
                            pe.wait_ge(w_lo, CHUNKS.index(("k", 0)) + 1)
                        w, col, lo, count, done = wk, u * HD, k_lo, NG * b + u + 1, k_mm
                    split_product(bank(lo, count)[:, :],
                                  [(lambda a, c=c: w[:, a, c, col:col + HD], lambda m, c=c: hT[0][:, m, c, :])
                                   for c in range(NC)], done)
                elif kind == "v":
                    if isinstance(b, int) and b == 0:
                        pe.wait_ge(w_lo, CHUNKS.index(("v", 0)) + 1)
                    pe.wait_ge(h_lo[0], NC * (b + 1))
                    split_product(bank(v_lo, 2 * NT * b + NT * u + v + 1)[:, 0:2 * HD],
                                  [(lambda a, c=c: hT[0][:, a, c, v * P:(v + 1) * P],
                                    lambda m, c=c: wv[:, m, c, u * 2 * HD:(u + 1) * 2 * HD])
                                   for c in range(NC)], v_mm)
                elif kind == "gu":
                    rows = P if u < FT - 1 else LAST_F
                    pe.wait_ge(h_lo[1], NC * (b + 1))
                    pe.wait_ge(piece_lo, (1 + (u * P + rows > HALF)) * NC + 2 * NC)
                    for name, read in (("gate", gu_gate), ("up", gu_hid)):
                        dst = bank(read, FT * b + u + 1)
                        w = wffn[name]
                        split_product(dst[0:rows, :],
                                      [(lambda a, c=c: w[:, a, c, u * P:u * P + rows],
                                        lambda m, c=c: hT[1][:, m, c, :]) for c in range(NC)], gu_mm)
                elif kind == "dn":
                    pe.wait_ge(hid_lo, FT * (b + 1))
                    pe.wait_ge(piece_lo, len(PIECES))
                    rows = [P if f < FT - 1 else LAST_F for f in range(FT)]
                    split_product(bank(dn_gate, NT * b + u + 1)[:, 0:HID],
                                  [(lambda a, f=f: hidT[0:rows[f], a, f, u * P:(u + 1) * P],
                                    lambda m, f=f: wffn["down"][0:rows[f], m, f, :]) for f in range(FT)], dn_mm)

            pe.wait_ge(wm_in, 16)
            pe.wait_ge(c_silu, 1)
            dst = bank(mod_out, 2)
            for m, kind in enumerate((0, 1, 3, 4)):
                for c in range(NC):
                    for k in range(NC):
                        mm = pe.matmul(dst[:, (m * NC + c) * NB:(m * NC + c + 1) * NB],
                                       wm[:, k, kind * HID + c * P:kind * HID + (c + 1) * P], csl[:, k, :],
                                       start=(k == 0), stop=(k == NC - 1))
            mm.then_inc(mod_mm, 1)
            pe.wait_ge(ident_set, 1)
            for kind, db, u, v in PROLOGUE:
                filler(kind, db, u, v)

            def attend(b, s, n, first):
                new, old = to_transpose(b, s, n, first), to_multiply(b, s, n, first)
                if new:
                    transposes(*new)
                if old:
                    values(*old)

            per_batch = {sc_max: NR * STEPS, v_lo: 2 * NT, o_add: STEPS, q_lo: NR * NG, k_lo: NG}
            start = []

            def slots(b, first, last):
                if not first:
                    if not entry:
                        entry.extend(users)
                        start.append(turn[0])
                    assert all(u is v for (u, _), (v, _) in zip(users, entry)) and (turn[0] - start[0]) % RING == 0
                    users[:] = [(u, n + per_batch[u] * (b - 1)) for u, n in entry]
                fill = fillers(first, last)
                for s in range(STEPS):
                    for n in range(NR):
                        scores(b, s, n)
                        attend(b, s, n, first)
                        for kind, db, u, v in share(fill[s], n):
                            filler(kind, b + db, u, v)

            def tail():
                for s in range(STEPS, STEPS + LAG_O):
                    for n in range(NR):
                        attend(NB - 1, s, n, False)
                    out_projection(NB - 1, s - LAG_O)
                for kind, _, u, v in TAIL:
                    filler(kind, NB - 1, u, v)

            batches(pe, slots, tail)

        @block.scalar
        def _(act):
            def high(dst, src, ready, count, done, scale=1.0):
                act.wait_ge(ready, count)
                act.activation(dst, src, ACT.Copy, scale=scale).then_inc(done, 1)

            def split_weight(n):
                kind, g = CHUNKS[n]
                dst = chunk_view(kind, g, 0)
                act.wait_ge(stage_in[n % 2], 16 * (n // 2 + 1))
                act.activation(dst, chunk_stage(kind, n), ACT.Copy, scale=SC).then_inc(w_hi, 1)

            def piece(n):
                kind, t, c0, cn, rows = PIECES[n]
                act.wait_ge(piece_w, n + 1)
                act.activation(wffn[kind][0:rows, 0, t, c0:c0 + cn],
                               pick[0:rows, 0, 0:cn].bitcast(F32), ACT.Copy).then_inc(piece_hi, 1)

            def normalise(which, b, i):
                if i == 0:
                    act.wait_ge(ln_nmr[which], b + 1)
                src = xn[0] if which == 0 else x1
                act.activation(xn[which][:, i, :], src[:, i, :], ACT.Identity, bias=nmr[:, which, i:i + 1],
                               scale=rstd[:, which, i:i + 1]).then_inc(ln_xn[which], 1)

            def filler(kind, b, u, v, turn):
                if kind in ("h1", "h2"):
                    which = int(kind == "h2")
                    act.wait_ge(h_mm[which], NC * b + u + 1)
                    if u == 0 and which == 0:
                        act.wait_ge(mod_out, 2)
                    if which == 1:
                        act.wait_ge(row_out, NB)
                    act.activation(hf[:, which, u, :], gen[turn][:, :], ACT.Identity,
                                   bias=modT[:, 2 * which, u, bass.ds(b, 1)],
                                   scale=modT[:, 2 * which + 1, u, bass.ds(b, 1)]).then_inc(h_f[which], 1)
                    act.wait_ge(h_f[which], NC * b + u + 1)
                    act.activation(hT[which][:, 0, u, :], hf[:, which, u, :], ACT.Copy).then_inc(h_hi[which], 1)
                elif kind == "q":
                    high(qT[:, u % 2, 0, v, :], gen[turn][:, :], q_mm, NR * (NG * b + u) + v + 1, q_hi, 1 / SC)
                elif kind == "k":
                    high(kT[:, u % 2, 0, :], gen[turn][:, :], k_mm, NG * b + u + 1, k_hi, 1 / SC)
                elif kind == "v":
                    high(vS[:, u, 0, v, :], gen[turn][:, 0:2 * HD], v_mm, 2 * NT * b + NT * u + v + 1, v_hi, 1 / SC)
                elif kind == "gu":
                    rows = P if u < FT - 1 else LAST_F
                    n = FT * b + u
                    act.wait_ge(gu_mm, 2 * n + 2)
                    if u >= 2:
                        act.wait_ge(hid_lo, n - 1)
                    act.activation(act_t[0:rows, u % 2, :], gen[turn][0:rows, :], ACT.Tanh,
                                   scale=0.5 / SC).then_inc(gu_tanh, 1)
                elif kind == "hh":
                    rows = P if u < FT - 1 else LAST_F
                    high(hidT[0:rows, 0, u, :], act_t[0:rows, u % 2, :], gu_hid, FT * b + u + 1, hid_hi)

            act.wait_ge(c_in, 16)
            act.activation(cth[:, :, :], cin[:, :, :], ACT.Tanh, scale=0.5).then_inc(c_tanh, 1)
            for i in range(NT):
                normalise(0, 0, i)
            turn = [1]
            for kind, db, u, v in PROLOGUE:
                if kind == "k":
                    split_weight(0)
                elif kind == "q" and v == 0:
                    split_weight(1)
                elif kind == "v" and v == 0:
                    split_weight(2)
                    split_weight(3)
                filler(kind, db, u, v, turn[0] % RING)
                turn[0] += banks_of(kind)

            def high_probs(b, s, j):
                kt = key_tile(b, s, j)
                ring = in_batch(s, j) % PTRING
                if not (isinstance(b, int) and kt < PTRING):
                    act.wait_ge(pv_mm, kt - PTRING + 1)
                high(pT[:, ring, 0, :], pt_ps[ring % 2][:, :], pt_mm, kt + 1, pt_hi, SC)

            def exponent(b, s, n):
                head = NR * (STEPS * b + s) + n
                keys = (TILE_OF[s % NT] + 1) * P
                act.wait_ge(sc_max, head + 1)
                p = prob[:, s % PRING, n, 0:keys]
                act.activation(p, p, ACT.Exp, bias=nmax[:, s % PRING, n:n + 1], scale=-1.0,
                               accum_out=rsum[:, s % PRING, n:n + 1]).then_inc(sc_exp, 1)

            def high_out(b, s):
                step = STEPS * b + s
                if not (isinstance(b, int) and step < 2):
                    act.wait_ge(o_mm, step - 1)
                high(oT[:, s % 2, 0, :, :], ot_ps[s % 2][:, :].rearrange("p (h n) -> p h n", h=NR),
                     pv_mm, key_tile(b, s, TILE_OF[s % NT]) + 1, ot_hi, 1 / SC)

            def attend(b, s, n, first):
                done, new = to_collect(b, s, n, first), to_transpose(b, s, n, first)
                if done:
                    high_out(*done)
                if new:
                    high_probs(*new)

            def slots(b, first, last):
                fill = fillers(first, last)
                for s in range(STEPS):
                    if first:
                        for n in CHUNK_SLOTS.get(s, []):
                            split_weight(n)
                    for n in range(NR):
                        attend(b, s, n, first)
                        exponent(b, s, n)
                        turn[0] += 1
                        if s == LN2_SLOT + 1 and not first:
                            normalise(1, b - 1, n)
                        if s == LN1_SLOT + 1 and not last:
                            normalise(0, b + 1, n)
                        for kind, db, u, v in share(fill[s], n):
                            filler(kind, b + db, u, v, turn[0] % RING)
                            turn[0] += banks_of(kind)
                    if first and s >= PIECE_SLOT0:
                        piece(s - PIECE_SLOT0)

            def tail():
                for s in range(STEPS, STEPS + LAG_O):
                    for n in range(NR):
                        attend(NB - 1, s, n, False)
                    turn[0] += 1
                for i in range(NT):
                    normalise(1, NB - 1, i)
                for kind, _, u, v in TAIL:
                    filler(kind, NB - 1, u, v, turn[0] % RING)
                    turn[0] += banks_of(kind)

            batches(act, slots, tail)

        @block.vector
        def _(dve):
            def hold():
                dve.nop(nofuse=True)

            def low(dst, src, hi, ready, count, done, scale):
                dve.wait_ge(ready, count)
                dve.scalar_tensor_tensor(out=dst, in0=src, scalar=scale, in1=hi,
                                         op0=ALU.mult, op1=ALU.subtract).then_inc(done, 1)

            def split_weight(n):
                kind, g = CHUNKS[n]
                low(chunk_view(kind, g, 1), chunk_stage(kind, n), chunk_view(kind, g, 0), w_hi, n + 1, w_lo, SC)

            lut_ops = [0]

            def chained(ins):
                lut_ops[0] += 1
                ins.then_inc(lut_step, 1)
                dve.wait_ge(lut_step, lut_ops[0])

            def piece(n):
                kind, t, c0, cn, rows = PIECES[n]
                dve.wait_ge(idx_in[n % 2], 16 * (n // 2 + 1))
                if n:
                    dve.wait_ge(piece_hi, n)
                src = idx[0:rows, n % 2, 0:cn]
                bit = [bits[0:rows, k, 0:cn] for k in range(3)]
                for k in range(3):
                    dve.tensor_scalar(bit[k], src, 2 << k, None, ALU.bitwise_and)
                chained(dve.tensor_scalar(src, src, 31, 31, ALU.logical_shift_left, ALU.arith_shift_right))

                def pair(slot, k):
                    chained(dve.tensor_scalar(pick[0:rows, slot, 0:cn], src, lutx[0:rows, k:k + 1],
                                              luts[0:rows, 2 * k:2 * k + 1].bitcast(I32),
                                              ALU.bitwise_and, ALU.bitwise_xor))

                def choose(slot, other, k):
                    chained(dve.copy_predicated(pick[0:rows, slot, 0:cn], bit[k], pick[0:rows, other, 0:cn]))

                for half in range(2):
                    top = half
                    pair(top, 4 * half)
                    pair(top + 1, 4 * half + 1)
                    choose(top, top + 1, 0)
                    pair(top + 1, 4 * half + 2)
                    pair(top + 2, 4 * half + 3)
                    choose(top + 1, top + 2, 0)
                    choose(top, top + 1, 1)
                dve.copy_predicated(pick[0:rows, 0, 0:cn], bit[2], pick[0:rows, 1, 0:cn]).then_inc(piece_w, 1)
                w = wffn[kind][0:rows, :, t, c0:c0 + cn]
                dve.wait_ge(piece_w, n + 1)
                dve.wait_ge(piece_hi, n + 1)
                dve.tensor_tensor(w[:, 1, :], pick[0:rows, 0, 0:cn].bitcast(F32), w[:, 0, :],
                                  ALU.subtract).then_inc(piece_lo, 1)

            def statistics(which, b, i):
                src = xn[0] if which == 0 else x1
                if which == 0 and i == 0:
                    dve.wait_ge(x_in, 16 * (b + 1))
                dve.bn_stats(stats[:, which, i, :], src[:, i, :]).then_inc(ln_stat[which], 1)
                dve.wait_ge(ln_stat[which], NT * b + i + 1)
                hold()
                dve.bn_aggr(mv[:, which, i, :], stats[:, which, i, :]).then_inc(ln_mv[which], 1)

            def variance(which, b):
                dve.wait_ge(ln_mv[which], NT * (b + 1))
                dve.tensor_scalar(mv[:, which, :, 0], mv[:, which, :, 0], -1.0, None, ALU.mult)
                dve.tensor_scalar(mv[:, which, :, 1], mv[:, which, :, 1], EPS, None, ALU.add).then_inc(ln_eps[which], 1)

            def out_add(b, s, turn):
                g, i = s // NT, TILE_OF[s % NT]
                step = STEPS * b + s
                dve.wait_ge(o_mm, step + 1)
                if isinstance(b, int) and b == 0 and s == 0:
                    dve.wait_ge(bo_in, 16)
                if g:
                    dve.wait_ge(o_add, step - NT + 1)
                dve.scalar_tensor_tensor(out=acc[:, i, :], in0=gen[turn][:, 0:HID], scalar=1 / SC,
                                         in1=(acc[:, i, :] if g else bo_row[:, :]),
                                         op0=ALU.mult, op1=ALU.add).then_inc(o_add, 1)
                if g == NG - 1:
                    dve.wait_ge(o_add, step + 1)
                    dve.tensor_tensor(acc[:, i, :], acc[:, i, :], row(b, 0), ALU.mult).then_inc(x1_gate, 1)
                    dve.wait_ge(x1_gate, NT * b + s % NT + 1)
                    if s % NT == 0:
                        dve.wait_ge(x1_in, 16 * (b + 1))
                    dve.tensor_tensor(x1[:, i, :], x1[:, i, :], acc[:, i, :], ALU.add).then_inc(x1_sum, 1)
                    dve.wait_ge(x1_sum, NT * b + s % NT + 1)
                    dve.bn_stats(stats[:, 1, i, :], x1[:, i, :]).then_inc(ln_stat[1], 1)
                    dve.wait_ge(ln_stat[1], NT * b + s % NT + 1)
                    hold()
                    dve.bn_aggr(mv[:, 1, i, :], stats[:, 1, i, :]).then_inc(ln_mv[1], 1)

            def row(b, which):
                return grow[:, bass.ds(b, 1), which, :].rearrange("p o n -> p (o n)")

            def filler(kind, b, u, v, turn):
                if kind == "o":
                    out_add(b, u, turn)
                elif kind == "q":
                    low(qT[:, u % 2, 1, v, :], gen[turn][:, :], qT[:, u % 2, 0, v, :],
                        q_hi, NR * (NG * b + u) + v + 1, q_lo, 1 / SC)
                elif kind == "k":
                    low(kT[:, u % 2, 1, :], gen[turn][:, :], kT[:, u % 2, 0, :], k_hi, NG * b + u + 1, k_lo, 1 / SC)
                elif kind == "v":
                    low(vS[:, u, 1, v, :], gen[turn][:, 0:2 * HD], vS[:, u, 0, v, :],
                        v_hi, 2 * NT * b + NT * u + v + 1, v_lo, 1 / SC)
                elif kind == "row":
                    dve.wait_ge(row_mm, u + 1)
                    sgn, mag = hf[:, 1, 0, :], hf[:, 1, 1, :]
                    dve.tensor_scalar(sgn, gen[turn][:, :], 0.0, 2.0, ALU.is_ge, ALU.mult).then_inc(row_sgn, 1)
                    dve.wait_ge(row_sgn, 4 * u + 1)
                    dve.scalar_tensor_tensor(out=mag, in0=sgn, scalar=-1.0, in1=gen[turn][:, :],
                                             op0=ALU.add, op1=ALU.mult).then_inc(row_sgn, 1)
                    dve.wait_ge(row_sgn, 4 * u + 2)
                    dve.tensor_scalar(mag, mag, GUARD, None, ALU.max).then_inc(row_sgn, 1)
                    dve.wait_ge(row_sgn, 4 * u + 3)
                    dve.scalar_tensor_tensor(out=grow[:, u, :, :].rearrange("p a n -> p (a n)"), in0=sgn, scalar=-1.0,
                                             in1=mag, op0=ALU.add, op1=ALU.mult).then_inc(row_sgn, 1)
                    dve.wait_ge(row_sgn, 4 * u + 4)
                    dve.tensor_scalar(grow[:, u, 1, :], grow[:, u, 1, :], 1 / SC, None, ALU.mult).then_inc(row_out, 1)
                elif kind == "gu":
                    rows = P if u < FT - 1 else LAST_F
                    n = FT * b + u
                    t = act_t[0:rows, u % 2, :]
                    dve.wait_ge(gu_tanh, n + 1)
                    dve.scalar_tensor_tensor(out=t, in0=t, scalar=1.0, in1=gen[turn][0:rows, :],
                                             op0=ALU.add, op1=ALU.mult).then_inc(gu_gate, 1)
                    dve.wait_ge(gu_gate, n + 1)
                    dve.scalar_tensor_tensor(out=t, in0=t, scalar=0.5 / (SC * SC), in1=gen[(turn + 1) % RING][0:rows, :],
                                             op0=ALU.mult, op1=ALU.mult).then_inc(gu_hid, 1)
                elif kind == "dn":
                    n = NT * b + u
                    dve.wait_ge(dn_mm, n + 1)
                    if u >= 2:
                        dve.wait_ge(out_sent[u % 2], 32 * b + 16 * (u // 2))
                    dve.tensor_tensor(outb[:, u % 2, :], gen[turn][:, 0:HID], row(b, 1), ALU.mult).then_inc(dn_gate, 1)
                    dve.wait_ge(dn_gate, n + 1)
                    dve.tensor_tensor(outb[:, u % 2, :], outb[:, u % 2, :], x1[:, u, :], ALU.add).then_inc(dn_out, 1)

            dve.wait_ge(c_tanh, 1)
            dve.scalar_tensor_tensor(out=cth[:, :, :], in0=cth[:, :, :], scalar=1.0, in1=cin[:, :, :],
                                     op0=ALU.add, op1=ALU.mult).then_inc(c_twice, 1)
            dve.wait_ge(c_twice, 1)
            dve.tensor_scalar(csl[:, :, :], cth[:, :, :], 0.5, None, ALU.mult).then_inc(c_silu, 1)
            dve.wait_ge(c_silu, 1)
            for i in range(NT):
                statistics(0, 0, i)
            variance(0, 0)
            dve.tensor_copy(crep[:, :, :, :], csl[:, :, :].unsqueeze(3).broadcast_to([P, NC, NB, P])).then_inc(c_rep, 1)
            dve.wait_ge(mod_mm, 1)
            md = gen[0][:, 0:4 * NC * NB].rearrange("p (m n) -> p m n", m=4)
            mt = modT[:, :, :, :].rearrange("p m c b -> p m (c b)")
            dve.tensor_copy(mt[:, 0:4:2, :], md[:, 0:4:2, :]).then_inc(mod_out, 1)
            dve.tensor_scalar(mt[:, 1:4:2, :], md[:, 1:4:2, :], 1.0, None, ALU.add).then_inc(mod_out, 1)
            turn = [1]
            for kind, db, u, v in PROLOGUE:
                if kind == "k":
                    split_weight(0)
                elif kind == "q" and v == 0:
                    split_weight(1)
                elif kind == "v" and v == 0:
                    split_weight(2)
                    split_weight(3)
                filler(kind, db, u, v, turn[0] % RING)
                turn[0] += banks_of(kind)

            def low_probs(b, s, j):
                ring = in_batch(s, j) % PTRING
                low(pT[:, ring, 1, :], pt_ps[ring % 2][:, :], pT[:, ring, 0, :], pt_hi, key_tile(b, s, j) + 1, pt_lo, SC)

            def maximum(b, s, n, first, turn):
                head = NR * (STEPS * b + s) + n
                keys = (TILE_OF[s % NT] + 1) * P
                dve.wait_ge(sc_mm, head + 1)
                if n == 0 and (s >= PRING or not first):
                    ob, os_ = (b, s - PRING) if s >= PRING else (b - 1, s - PRING + STEPS)
                    dve.wait_ge(pt_mm, key_tile(ob, os_, TILE_OF[os_ % NT]) + 1)
                if first and s == 0 and n == 0:
                    dve.wait_ge(mask_set, 1)
                if first and s == 2 and n == 0:
                    dve.wait_ge(row_mm, NB)
                hold()
                dve.tensor_tensor_reduce(out=prob[:, s % PRING, n, 0:keys], in0=gen[turn][:, 0:keys],
                                         in1=mask[:, S - keys:S], scale=-1.0, scalar=-NEG, op0=ALU.add, op1=ALU.min,
                                         accum_out=nmax[:, s % PRING, n:n + 1]).then_inc(sc_max, 1)

            def inverse(b, s):
                step = STEPS * b + s
                dve.wait_ge(sc_exp, NR * (step + 1))
                if not (isinstance(b, int) and step < PRING):
                    dve.wait_ge(p_norm, step - PRING + 1)
                dve.reciprocal(rinv[:, s % PRING, :], rsum[:, s % PRING, :]).then_inc(p_inv, 1)

            def low_out(b, s):
                low(oT[:, s % 2, 1, :, :], ot_ps[s % 2][:, :].rearrange("p (h n) -> p h n", h=NR), oT[:, s % 2, 0, :, :],
                    ot_hi, STEPS * b + s + 1, ot_lo, 1 / SC)

            def attend(b, s, n, first):
                done, new = to_collect(b, s, n, first), to_transpose(b, s, n, first)
                if done:
                    low_out(*done)
                if new:
                    low_probs(*new)

            def slots(b, first, last):
                fill = fillers(first, last)
                for s in range(STEPS):
                    if first:
                        for n in CHUNK_SLOTS.get(s, []):
                            split_weight(n)
                    for n in range(NR):
                        maximum(b, s, n, first, turn[0] % RING)
                        turn[0] += 1
                        if n == 0 and not (first and s == 0):
                            inverse(*((b, s - 1) if s else (b - 1, STEPS - 1)))
                        attend(b, s, n, first)
                        for kind, db, u, v in share(fill[s], n):
                            filler(kind, b + db, u, v, turn[0] % RING)
                            turn[0] += banks_of(kind)
                    if first and s == 0:
                        dve.wait_ge(lut_in, 16)
                        chained(dve.tensor_scalar(luts[:, :], lutb[:, :], SC, None, ALU.mult))
                        li = luts[:, :].bitcast(I32).rearrange("p (k two) -> p k two", two=2)
                        chained(dve.tensor_tensor(lutx[:, :], li[:, :, 0], li[:, :, 1], ALU.bitwise_xor))
                    if first and s >= PIECE_SLOT0:
                        piece(s - PIECE_SLOT0)
                    if s == LN2_SLOT and not first:
                        variance(1, b - 1)
                    if LN1_SLOT - NT <= s < LN1_SLOT and not last:
                        statistics(0, b + 1, s - LN1_SLOT + NT)
                    if s == LN1_SLOT and not last:
                        variance(0, b + 1)

            def tail():
                inverse(NB - 1, STEPS - 1)
                for s in range(STEPS, STEPS + LAG_O):
                    for n in range(NR):
                        attend(NB - 1, s, n, False)
                    out_add(NB - 1, s - LAG_O, turn[0] % RING)
                    turn[0] += 1
                variance(1, NB - 1)
                for kind, _, u, v in TAIL:
                    filler(kind, NB - 1, u, v, turn[0] % RING)
                    turn[0] += banks_of(kind)

            batches(dve, slots, tail)

        @block.gpsimd
        def _(pool):
            pool.memset(ident[:, :], 0.0).then_inc(ident_0, 1)
            pool.wait_ge(ident_0, 1)
            pool.affine_select(out=ident[:, :], in_=ident[:, :], compare_op=ALU.not_equal, fill=1.0, base=0,
                               pattern=[[-1, P]], channel_multiplier=1).then_inc(ident_set, 1)
            pool.memset(mhalf[:, :], -0.5).then_inc(half_set, 1)
            pool.wait_ge(half_set, 1)

            def root(which, b):
                pool.wait_ge(ln_eps[which], b + 1)
                if not (isinstance(b, int) and b == 0):
                    pool.wait_ge(ln_xn[which], NT * b)
                pool.tensor_tensor(rstd[:, which, :], mv[:, which, :, 1], mhalf[:, :], ALU.pow).then_inc(ln_rstd[which], 1)
                pool.wait_ge(ln_rstd[which], b + 1)
                pool.tensor_tensor(nmr[:, which, :], mv[:, which, :, 0], rstd[:, which, :], ALU.mult).then_inc(ln_nmr[which], 1)

            def filler(kind, b, u, v):
                if kind in ("h1", "h2"):
                    which = int(kind == "h2")
                    pool.wait_ge(h_hi[which], NC * b + u + 1)
                    pool.tensor_tensor(hT[which][:, 1, u, :], hf[:, which, u, :], hT[which][:, 0, u, :],
                                       ALU.subtract).then_inc(h_lo[which], 1)
                elif kind == "hh":
                    rows = P if u < FT - 1 else LAST_F
                    pool.wait_ge(hid_hi, FT * b + u + 1)
                    pool.tensor_tensor(hidT[0:rows, 1, u, :], act_t[0:rows, u % 2, :], hidT[0:rows, 0, u, :],
                                       ALU.subtract).then_inc(hid_lo, 1)

            def divide(b, s):
                keys = (TILE_OF[s % NT] + 1) * P
                pool.wait_ge(p_inv, STEPS * b + s + 1)
                p = prob[:, s % PRING, :, 0:keys]
                pool.tensor_tensor(p, p, rinv[:, s % PRING, :].unsqueeze(2).broadcast_to([P, NR, keys]),
                                   ALU.mult).then_inc(p_norm, 1)

            root(0, 0)
            pool.memset(mask[:, :], 0.0).then_inc(mask_0, 1)
            pool.wait_ge(mask_0, 1)
            pool.affine_select(out=mask[:, S - P:S], in_=mask[:, S - P:S], compare_op=ALU.is_ge, fill=NEG, base=0,
                               pattern=[[-1, P]], channel_multiplier=1).then_inc(mask_set, 1)
            for kind, db, u, v in PROLOGUE:
                filler(kind, db, u, v)

            def slots(b, first, last):
                fill = fillers(first, last)
                for s in range(STEPS):
                    if not (first and s == 0):
                        divide(*((b, s - 1) if s else (b - 1, STEPS - 1)))
                    for n in range(NR):
                        for kind, db, u, v in share(fill[s], n):
                            filler(kind, b + db, u, v)
                    if s == LN2_SLOT and not first:
                        root(1, b - 1)
                    if s == LN1_SLOT and not last:
                        root(0, b + 1)

            def tail():
                divide(NB - 1, STEPS - 1)
                root(1, NB - 1)
                for kind, _, u, v in TAIL:
                    filler(kind, NB - 1, u, v)

            batches(pool, slots, tail)


_INS = [("x", "L0_attn_hidden_states"), ("wqT", "L0_attn_Wq"), ("wkT", "L0_attn_Wk"), ("wvT", "L0_attn_Wv"),
        ("woT", "L0_attn_Wo"), ("bo", "L0_attn_bo"), ("lut", "L0_ffn_lut"), ("gate_iT", "L0_ffn_gate_idx"),
        ("up_iT", "L0_ffn_up_idx"), ("down_iT", "L0_ffn_down_idx"), ("cT", "L0_c"), ("wmod", "L0_wmod")]


def kernel(**inputs):
    import numpy as np
    import concourse.bacc as bacc
    from concourse.bass_utils import run_bass_kernel_spmd as run

    nc = bacc.Bacc("TRN2", target_bir_lowering=False, num_devices=1)
    arrays, args = {}, []
    for short, name in _INS:
        a = np.asarray(inputs[name])
        a = np.ascontiguousarray(a.T if short.endswith("T") else a)
        arrays[short] = a
        args.append(nc.dram_tensor(short, a.shape, mybir.dt.from_np(a.dtype), kind="ExternalInput").ap())
    args.append(nc.dram_tensor("y", (NB, S, HID), F32, kind="ExternalOutput").ap())
    block_program(nc, *args)
    return run(nc, [arrays], core_ids=[0]).results[0]["y"]
```

```python
from contextlib import ExitStack

import concourse.bass as bass
from concourse import mybir

F32 = mybir.dt.float32
F16 = mybir.dt.float16
I32 = mybir.dt.int32
ALU = mybir.AluOpType
ACT = mybir.ActivationFunctionType

P = 128
NB, S, HID = 4, 512, 256
NG, NR, HD = 4, 4, 128
NT = S // P
NC = HID // P
NQ = NG * NR * HD
INTER = 688
FT = -(-INTER // P)
LAST_F = INTER - (FT - 1) * P
LUT = 16
STEPS = NG * NT
EPS = 1e-5
NEG = -3e38
SC = 64.0
GUARD = 0.25

TILE_OF = [3, 0, 2, 1]
OFF = [sum(TILE_OF[m] + 1 for m in range(r)) for r in range(NT)]
KT = sum(t + 1 for t in range(NT))
LAG_PV, LAG_O = 2, 3
PRING = 4
PTRING = 4
RING = 4

CHUNKS = [("k", 0), ("q", 0), ("v", 0), ("q", 1), ("o", 0), ("q", 2), ("o", 1), ("q", 3), ("o", 2), ("o", 3)]
CHUNKS_EARLY = 4
CHUNK_SLOTS = {1: [4], 2: [5], 4: [6], 5: [7], 7: [8], 8: [9]}
CH = NC * 512

HALF = INTER // 2
PIECES = ([("gate", c, h * HALF, HALF, P) for h in range(2) for c in range(NC)]
          + [("up", c, h * HALF, HALF, P) for h in range(2) for c in range(NC)]
          + [("down", f, 0, HID, P if f < FT - 1 else LAST_F) for f in range(FT)])

PERIOD = 10
ON_DVE = [(-10, "bit0"), (-4, "bit1"), (-2, "bit2"), (0, "choose01"), (1, "choose23"), (2, "choose02"),
          (4, "choose45"), (5, "choose67"), (7, "choose46"), (9, "choose04")]
ON_ACT = [(-2, "pair3"), (0, "pair6"), (1, "pair7"), (3, "bit3"), (12, "high")]
ON_POOL = [(-6, "pair4"), (-5, "pair0"), (-4, "pair1"), (-3, "pair2"), (-1, "pair5"), (14, "low")]
MASK_BIT = {"choose01": 1, "choose23": 1, "choose45": 1, "choose67": 1, "choose02": 2, "choose46": 2, "choose04": 3}


def in_order(ops):
    return sorted((PERIOD * n + at, op, n) for n in range(len(PIECES)) for at, op in ops)


DVE_LOOKUPS, ACT_LOOKUPS, POOL_LOOKUPS = in_order(ON_DVE), in_order(ON_ACT), in_order(ON_POOL)
LOOKUP_BEGIN, LOOKUP_END = DVE_LOOKUPS[0][0], POOL_LOOKUPS[-1][0] + 1
LOOKUP_SLOT = 1


def lookups(ops, s, n):
    quarters, q = NR * (STEPS - LOOKUP_SLOT), NR * (s - LOOKUP_SLOT) + n
    return [o for o in ops if (o[0] - LOOKUP_BEGIN) * quarters // (LOOKUP_END - LOOKUP_BEGIN) == q]


def done(ops, name, piece):
    return [o[1:] for o in ops].index((name, piece)) + 1


LN2_SLOT = 3
LN1_SLOT = 9


def gu_items(w):
    items = [("gu", w, 0, 0)]
    for n in range(1, FT):
        items += [("gu", w, n, 0), ("hh", w, n - 1, 0)]
    return items + [("hh", w, FT - 1, 0)]


def q_items(w, g):
    return [("k", w, g, 0)] + [("q", w, g, h) for h in range(NR)]


def fillers(first, last):
    f = [[] for _ in range(STEPS)]

    def put(slots, items):
        for n, it in enumerate(items):
            f[slots[n * len(slots) // len(items)]].append(it)

    put([0, 1, 2, 3], q_items(0, 1))
    put([4, 5, 6, 7], q_items(0, 2))
    put([5, 6, 7], [("v", 0, 1, t) for t in range(NT)])
    put([8, 9, 10], q_items(0, 3))
    if first:
        put([0, 1], [("mod", 0, 1, 0)] + [("row", 0, b, 0) for b in range(NB)])
        put([1], [("v", 0, 0, t) for t in range(NT)])
    else:
        put([5], [("h2", -1, c, 0) for c in range(NC)])
        put([6, 7, 8, 9, 10], gu_items(-1))
        put([11, 12, 13], [("dn", -1, i, 0) for i in range(NT)])
    if not last:
        put([11], [("h1", 1, c, 0) for c in range(NC)])
        put([12, 13, 14], q_items(1, 0))
        put([15], [("v", 1, 0, t) for t in range(NT)])
    return f


PROLOGUE = [("mod", 0, 0, 0)] + [("h1", 0, c, 3) for c in range(NC)] + q_items(0, 0)
TAIL = [("h2", 0, c, part) for part in (1, 2) for c in range(NC)] + gu_items(0)
TAIL += [("dn", 0, i, part) for part in (1, 2) for i in range(NT - 1)] + [("dn", 0, NT - 1, 0)]


def banks_of(kind, part):
    if kind == "hh" or kind in ("h2", "dn") and part == 2:
        return 0
    return 2 if kind == "gu" else 1


def begun(kind, u, turn):
    return (turn - (NT - 1 if kind == "dn" else NC) + u) % RING


def share(items, n):
    return [it for k, it in enumerate(items) if -(-(k + 1) * NR // (len(items) + 1)) - 1 == n]


def back(b, s, k, first):
    if s - k >= STEPS or (first and s < k):
        return None
    return (b, s - k) if s >= k else (b - 1, s - k + STEPS)


def to_transpose(b, s, n, first):
    old = back(b, s, LAG_PV, first)
    return (*old, n) if old and n <= TILE_OF[old[1] % NT] else None


def to_multiply(b, s, n, first):
    return to_transpose(b, s, n - 2, first) if n >= 2 else to_transpose(b, s - 1, n + 2, first) if s else (
        None if first else to_transpose(b - 1, STEPS - 1, n + 2, False))


def to_collect(b, s, n, first):
    for k, at in ((LAG_PV, n), (LAG_PV + 1, n + NR)):
        old = back(b, s, k, first)
        if old and at == TILE_OF[old[1] % NT] + 3:
            return old
    return None


def to_project(b, s, n, first):
    if n not in (NR - 1, 0):
        return None
    old = back(b, s, LAG_O if n else LAG_O + 1, first)
    return old if old and (TILE_OF[old[1] % NT] == NT - 1) == (n == 0) else None


def in_batch(s, j):
    return (s // NT) * KT + OFF[s % NT] + j


def key_tile(b, s, j):
    return b * (NG * KT) + in_batch(s, j)


def block_program(nc, x, wqT, wkT, wvT, woT, bo, lut, gate_iT, up_iT, down_iT, cT, wmod, out):
    with ExitStack() as ctx:
        def sb(name, shape, dt):
            return ctx.enter_context(nc.sbuf_tensor(name, shape, dt))

        def ps(name):
            return ctx.enter_context(nc.psum_tensor(name, [P, 512], F32))

        def sem(name):
            return ctx.enter_context(nc.semaphore(name))

        wq = sb("wq", [P, 2, NC, NQ], F16)
        wk = sb("wk", [P, 2, NC, NG * HD], F16)
        wv = sb("wv", [P, 2, NC, NG * HD], F16)
        wo = sb("wo", [P, 2, NG * NR, HID], F16)
        wffn = {"gate": sb("wg", [P, 2, NC, INTER], F16), "up": sb("wu", [P, 2, NC, INTER], F16),
                "down": sb("wd", [P, 2, FT, HID], F16)}
        hT = [sb("h1T", [P, 2, NC, S], F16), sb("h2T", [P, 2, NC, S], F16)]
        qT = sb("qT", [P, 2, 2, NR, S], F16)
        kT = sb("kT", [P, 2, 2, S], F16)
        vS = sb("vS", [P, 2, 2, NT, 2 * HD], F16)
        pT = sb("pT", [P, PTRING, 2, NR * P], F16)
        oT = sb("oT", [P, 2, 2, NR, P], F16)
        hidT = sb("hidT", [P, 2, FT, S], F16)
        prob = sb("prob", [P, PRING, NR, S], F32)
        nmax = sb("nmax", [P, PRING, NR], F32)
        rsum = sb("rsum", [P, PRING, NR], F32)
        rinv = sb("rinv", [P, PRING, NR], F32)
        xn = [sb("xn1", [P, NT, HID], F32), sb("xn2", [P, NT, HID], F32)]
        x1 = sb("x1", [P, NT, HID], F32)
        acc = sb("acc", [P, NT, HID], F32)
        outb = sb("outb", [P, 2, HID], F32)
        hf = sb("hf", [P, 2, NC, S], F32)
        act_t = sb("act_t", [P, 2, S], F32)
        stats = sb("stats", [P, 2, NT, 6], F32)
        mv = sb("mv", [P, 2, NT, 2], F32)
        rstd = sb("rstd", [P, 2, NT], F32)
        nmr = sb("nmr", [P, 2, NT], F32)
        modT = sb("modT", [P, 4, NC, NB], F32)
        grow = sb("grow", [P, NB, 2, HID], F32)
        bo_row = sb("bo_row", [P, HID], F32)
        early = prob[:, 0:2, :, :].rearrange("p a h n -> p (a h n)")
        ident = sb("ident", [P, P], F32)
        mask = sb("mask", [P, S], F32)
        mhalf = sb("mhalf", [P, NT], F32)
        stage = sb("stage", [P, 2, CH], F32)
        idx = sb("idx", [P, 2, HALF], I32)
        spare = hidT[:, :, :, :].rearrange("p a f s -> p (a f s)").bitcast(F32)
        spare = [spare[:, k * HALF:(k + 1) * HALF] for k in range(8)]
        more = hT[1][:, :, :, :].rearrange("p a c s -> p (a c s)").bitcast(F32)
        more = [more[:, k * HALF:(k + 1) * HALF] for k in range(2)]
        half_t = [act_t[:, k, 0:HALF] for k in range(2)]
        half_x = [xn[1][:, k:k + 2, :].rearrange("p t n -> p (t n)")[:, 0:HALF] for k in (0, 2)]
        half_o = outb[:, :, :].rearrange("p a n -> p (a n)")[:, 0:HALF]
        slot_of = [spare[0:2]] + [[spare[k + 1]] * 2 for k in range(1, 4)] + [spare[5:7], [spare[7]] * 2,
                                                                              [half_t[0]] * 2, [half_o] * 2]
        bits = [[m.bitcast(I32) for m in pair] for pair in (more, [half_t[1]] * 2, [half_x[0]] * 2, [half_x[1]] * 2)]
        lutb = sb("lutb", [P, LUT], F32)
        lutd = sb("lutd", [P, LUT // 2], F32)
        minus_7 = sb("minus_7", [P, 1], F32)
        cin = sb("cin", [P, NC, NB], F32)
        cth = sb("cth", [P, NC, NB], F32)
        csl = sb("csl", [P, NC, NB], F32)
        flat = prob[:, 2:4, :, :].rearrange("p a h n -> p (a h n)")
        wm = flat[:, 0:NC * 6 * HID].rearrange("p (c n) -> p c n", c=NC)
        crep = flat[:, NC * 6 * HID:NC * 6 * HID + NC * NB * P].rearrange("p (c b n) -> p c b n", c=NC, b=NB)

        pt_ps = [ps("pt0"), ps("pt1")]
        ot_ps = [ps("ot0"), ps("ot1")]
        gen = [ps(f"gen{n}") for n in range(RING)]

        ident_set, mask_set, half_set, ident_0, mask_0 = (sem(n) for n in
                                                          ("ident_set", "mask_set", "half_set", "ident_0", "mask_0"))
        c_in, wm1_in, wm_in, lut_in, bo_in = (sem(n) for n in ("c_in", "wm1_in", "wm_in", "lut_in", "bo_in"))
        x_in, x1_in = sem("x_in"), sem("x1_in")
        early_in = [sem(f"early_in{n}") for n in range(CHUNKS_EARLY)]
        stage_in = [sem("stage_in0"), sem("stage_in1")]
        idx_in = [sem("idx_in0"), sem("idx_in1")]
        out_sent = [sem("out_sent0"), sem("out_sent1")]
        c_tanh, c_twice, c_silu, c_rep, mod_mm, mod_out = (sem(n) for n in
                                                           ("c_tanh", "c_twice", "c_silu", "c_rep", "mod_mm", "mod_out"))
        row_mm, row_sgn, row_out = sem("row_mm"), sem("row_sgn"), sem("row_out")
        w_hi, w_lo = sem("w_hi"), sem("w_lo")
        lut_table, lut_dve, lut_act, lut_pool, minus_7_set = (sem(n) for n in
                                                           ("lut_table", "lut_dve", "lut_act", "lut_pool", "minus_7_set"))
        sc_mm, sc_max, sc_exp, p_inv, p_norm = (sem(n) for n in
                                                      ("sc_mm", "sc_max", "sc_exp", "p_inv", "p_norm"))
        pt_mm, pt_hi, pt_lo, pv_mm = sem("pt_mm"), sem("pt_hi"), sem("pt_lo"), sem("pv_mm")
        ot_hi, ot_lo, o_mm, o_add = sem("ot_hi"), sem("ot_lo"), sem("o_mm"), sem("o_add")
        q_mm, q_hi, q_lo = sem("q_mm"), sem("q_hi"), sem("q_lo")
        k_mm, k_hi, k_lo = sem("k_mm"), sem("k_hi"), sem("k_lo")
        v_mm, v_hi, v_lo = sem("v_mm"), sem("v_hi"), sem("v_lo")
        ln_stat = [sem("ln1_stat"), sem("ln2_stat")]
        ln_mv = [sem("ln1_mv"), sem("ln2_mv")]
        ln_eps = [sem("ln1_eps"), sem("ln2_eps")]
        ln_rstd = [sem("ln1_rstd"), sem("ln2_rstd")]
        ln_nmr = [sem("ln1_nmr"), sem("ln2_nmr")]
        ln_xn = [sem("ln1_xn"), sem("ln2_xn")]
        h_mm = [sem("h1_mm"), sem("h2_mm")]
        h_f = [sem("h1_f"), sem("h2_f")]
        h_hi = [sem("h1_hi"), sem("h2_hi")]
        h_lo = [sem("h1_lo"), sem("h2_lo")]
        x1_gate, x1_sum = sem("x1_gate"), sem("x1_sum")
        gu_mm, gu_tanh, gu_gate, gu_hid, hid_hi, hid_lo = (sem(n) for n in
                                                           ("gu_mm", "gu_tanh", "gu_gate", "gu_hid", "hid_hi", "hid_lo"))
        dn_mm, dn_gate, dn_out = sem("dn_mm"), sem("dn_gate"), sem("dn_out")

        block = ctx.enter_context(nc.Block())

        def chunk_view(kind, g, part):
            if kind == "o":
                return wo[:, part, g * NR:(g + 1) * NR, :]
            return {"q": wq, "k": wk, "v": wv}[kind][:, part, :, g * 512:(g + 1) * 512]

        def chunk_at(n):
            if n < CHUNKS_EARLY:
                return early[:, n * CH:(n + 1) * CH], early_in[n], 16
            m = n - CHUNKS_EARLY
            return stage[:, m % 2, :], stage_in[m % 2], 16 * (m // 2 + 1)

        def chunk_stage(kind, n):
            return chunk_at(n)[0].rearrange("p (a n) -> p a n", a=NR if kind == "o" else NC)

        def batches(eng, slots, tail):
            slots(0, True, False)
            with eng.Fori(1, NB - 1) as b:
                slots(b, False, False)
            slots(NB - 1, False, True)
            tail()

        @block.sync
        def _(sp):
            def load_chunk(n):
                kind, g = CHUNKS[n]
                if n >= CHUNKS_EARLY + 2:
                    sp.wait_ge(w_lo, n - 1)
                dst, there, _ = chunk_at(n)
                if kind == "o":
                    src = woT[g * NR * HD:(g + 1) * NR * HD, :].rearrange("(h d) n -> d h n", d=HD)
                    dst = dst.rearrange("p (h n) -> p h n", h=NR)
                else:
                    w = {"q": wqT, "k": wkT, "v": wvT}[kind]
                    src = w[:, g * 512:(g + 1) * 512].rearrange("(c p) n -> p c n", p=P)
                    dst = dst.rearrange("p (c n) -> p c n", c=NC)
                sp.dma_start(dst, src).then_inc(there, 16)

            def load_piece(n):
                kind, t, c0, cn, rows = PIECES[n]
                if n >= 2:
                    sp.wait_ge(lut_dve, done(DVE_LOOKUPS, "bit2", n - 2))
                    sp.wait_ge(lut_act, done(ACT_LOOKUPS, "bit3", n - 2))
                src = {"gate": gate_iT, "up": up_iT, "down": down_iT}[kind]
                sp.dma_start(idx[0:rows, n % 2, 0:cn], src[t * P:t * P + rows, c0:c0 + cn]).then_inc(idx_in[n % 2], 16)

            def load_x(b):
                sp.dma_start(xn[0][:, :, :], x[b].rearrange("(t p) n -> p t n", p=P)).then_inc(x_in, 16)

            def store(b, i):
                sp.wait_ge(dn_out, NT * b + i + 1)
                sp.dma_start(out[b, i * P:(i + 1) * P, :], outb[:, i % 2, :]).then_inc(out_sent[i % 2], 16)

            sp.dma_start(cin[:, :, :], cT.rearrange("(c p) b -> p c b", p=P)).then_inc(c_in, 16)
            load_x(0)
            wv_d = wmod.rearrange("(c p) n -> p c n", p=P)
            sp.dma_start(wm[:, :, 0:2 * HID], wv_d[:, :, 0:2 * HID]).then_inc(wm1_in, 16)
            for n in range(2):
                load_chunk(n)
            sp.dma_start(wm[:, :, 2 * HID:6 * HID], wv_d[:, :, 2 * HID:6 * HID]).then_inc(wm_in, 16)
            for n in range(2, CHUNKS_EARLY + 2):
                load_chunk(n)
            sp.dma_start(bo_row[:, :], bo.rearrange("(o n) -> o n", o=1).broadcast_to([P, HID])).then_inc(bo_in, 16)
            sp.dma_start(lutb[:, :], lut.rearrange("(o n) -> o n", o=1).broadcast_to([P, LUT])).then_inc(lut_in, 16)

            def slots(b, first, last):
                if not last:
                    sp.wait_ge(h_mm[0], NC * b + NC)
                    load_x(b + 1)
                if first:
                    sp.dma_start(x1[:, :, :], x[b].rearrange("(t p) n -> p t n", p=P)).then_inc(x1_in, 16)
                    load_piece(0)
                    load_piece(1)
                    for s in range(STEPS):
                        for n in CHUNK_SLOTS.get(s, []):
                            if n >= CHUNKS_EARLY + 2:
                                load_chunk(n)
                        for q in range(NR):
                            for _, op, n in lookups(ACT_LOOKUPS, s, q):
                                if op == "bit3" and n + 2 < len(PIECES):
                                    load_piece(n + 2)
                else:
                    for i in range(NT):
                        store(b - 1, i)
                    for r in range(2):
                        sp.wait_ge(out_sent[r], 16 * NT // 2 * b)
                    sp.dma_start(x1[:, :, :], x[b].rearrange("(t p) n -> p t n", p=P)).then_inc(x1_in, 16)

            def tail():
                for i in range(NT):
                    store(NB - 1, i)
                for r in range(2):
                    sp.wait_ge(out_sent[r], 16 * NB * NT // 2)

            batches(sp, slots, tail)

        @block.tensor
        def _(pe):
            users = [None] * RING
            entry = []
            turn = [0]

            def bank(sem_read, count):
                n = turn[0] % RING
                if users[n] is not None:
                    pe.wait_ge(*users[n])
                users[n] = (sem_read, count)
                turn[0] += 1
                return gen[n]

            def split_product(dst, pairs, done, ready=None):
                last = None
                for n, (w, m) in enumerate(pairs):
                    if ready:
                        pe.wait_ge(ready[0], ready[1] + n)
                    for k, (a, c) in enumerate(((0, 0), (0, 1), (1, 0))):
                        last = pe.matmul(dst, w(a), m(c), start=(n == 0 and k == 0),
                                         stop=(n == len(pairs) - 1 and k == 2))
                last.then_inc(done, 1)

            def scores(b, s, n):
                g, i = s // NT, TILE_OF[s % NT]
                head = NR * (STEPS * b + s) + n
                pe.wait_ge(q_lo, NR * (NG * b + g) + n + 1)
                if n == 0:
                    pe.wait_ge(k_lo, NG * b + g + 1)
                split_product(bank(sc_max, head + 1)[:, 0:(i + 1) * P],
                              [(lambda a: qT[:, g % 2, a, n, i * P:(i + 1) * P],
                                lambda c: kT[:, g % 2, c, 0:(i + 1) * P])], sc_mm)

            def transposes(b, s, j):
                kt = key_tile(b, s, j)
                if j == 0:
                    pe.wait_ge(p_norm, STEPS * b + s + 1)
                ring = in_batch(s, j) % 2
                if not (isinstance(b, int) and kt < 2):
                    pe.wait_ge(pt_lo, kt - 1)
                for n in range(NR):
                    t = pe.transpose(pt_ps[ring][:, n * P:(n + 1) * P],
                                     prob[:, s % PRING, n, j * P:(j + 1) * P], ident[:, :])
                t.then_inc(pt_mm, 1)

            def values(b, s, j):
                g, i = s // NT, TILE_OF[s % NT]
                step = STEPS * b + s
                pe.wait_ge(pt_lo, key_tile(b, s, j) + 1)
                pe.wait_ge(v_lo, 2 * NT * b + NT * (g // 2) + j + 1)
                if j == 0 and not (isinstance(b, int) and step < 2):
                    pe.wait_ge(ot_lo, step - 1)
                ring = in_batch(s, j) % PTRING
                for k, (a, c) in enumerate(((0, 0), (0, 1), (1, 0))):
                    mm = pe.matmul(ot_ps[s % 2][:, :], vS[:, g // 2, a, j, (g % 2) * HD:(g % 2 + 1) * HD],
                                   pT[:, ring, c, :], start=(j == 0 and k == 0), stop=(j == i and k == 2))
                mm.then_inc(pv_mm, 1)

            def out_projection(b, s):
                step, g = STEPS * b + s, s // NT
                pe.wait_ge(ot_lo, step + 1)
                if isinstance(b, int) and b == 0:
                    pe.wait_ge(w_lo, CHUNKS.index(("o", g)) + 1)
                split_product(bank(o_add, step + 1)[:, 0:HID],
                              [(lambda a, n=n: oT[:, s % 2, a, n, :], lambda c, n=n: wo[:, c, g * NR + n, :])
                               for n in range(NR)], o_mm)

            def filler(kind, b, u, v):
                if kind == "mod":
                    dst = bank(mod_out, 2 * u + 2)
                    pe.wait_ge(wm_in if u else wm1_in, 16)
                    pe.wait_ge(c_silu, 1)
                    for m in range(2):
                        col = (3 * u + m) * HID
                        for c in range(NC):
                            for k in range(NC):
                                mm = pe.matmul(dst[:, (m * NC + c) * NB:(m * NC + c + 1) * NB],
                                               wm[:, k, col + c * P:col + (c + 1) * P], csl[:, k, :],
                                               start=(k == 0), stop=(k == NC - 1))
                    mm.then_inc(mod_mm, 1)
                elif kind == "row":
                    dst = bank(row_sgn, 4 * u + 2)
                    if u == 0:
                        pe.wait_ge(c_rep, 1)
                        pe.wait_ge(wm_in, 16)
                    for half, col in ((0, 2 * HID), (1, 5 * HID)):
                        for c in range(NC):
                            mm = pe.matmul(dst[:, half * HID:(half + 1) * HID], crep[:, c, u, :],
                                           wm[:, c, col:col + HID], start=(c == 0), stop=(c == NC - 1))
                    mm.then_inc(row_mm, 1)
                elif kind in ("h1", "h2"):
                    which = int(kind == "h2")
                    dst = gen[begun(kind, u, turn[0])] if v == 2 else bank(h_f[which], NC * b + u + 1)
                    for k in {1: range(NT - 1), 2: range(NT - 1, NT)}.get(v, range(NT)):
                        pe.wait_ge(ln_xn[which], NT * b + k + 1 if v in (1, 2) else NT * (b + 1))
                        t = TILE_OF[k]
                        mm = pe.transpose(dst[:, t * P:(t + 1) * P], xn[which][:, t, u * P:(u + 1) * P], ident[:, :])
                    if v != 1:
                        mm.then_inc(h_mm[which], 1)
                elif kind in ("q", "k"):
                    if kind == "q":
                        if isinstance(b, int) and b == 0:
                            pe.wait_ge(w_lo, CHUNKS.index(("q", u)) + 1)
                        w, col, lo, count, done = wq, (u * NR + v) * HD, q_lo, NR * (NG * b + u) + v + 1, q_mm
                    else:
                        if isinstance(b, int) and b == 0:
                            pe.wait_ge(w_lo, CHUNKS.index(("k", 0)) + 1)
                        w, col, lo, count, done = wk, u * HD, k_lo, NG * b + u + 1, k_mm
                    split_product(bank(lo, count)[:, :],
                                  [(lambda a, c=c: w[:, a, c, col:col + HD], lambda m, c=c: hT[0][:, m, c, :])
                                   for c in range(NC)], done, (h_lo[0], NC * b + 1))
                elif kind == "v":
                    if isinstance(b, int) and b == 0:
                        pe.wait_ge(w_lo, CHUNKS.index(("v", 0)) + 1)
                    split_product(bank(v_lo, 2 * NT * b + NT * u + v + 1)[:, 0:2 * HD],
                                  [(lambda a, c=c: hT[0][:, a, c, v * P:(v + 1) * P],
                                    lambda m, c=c: wv[:, m, c, u * 2 * HD:(u + 1) * 2 * HD])
                                   for c in range(NC)], v_mm, (h_lo[0], NC * b + 1))
                elif kind == "gu":
                    rows = P if u < FT - 1 else LAST_F
                    pe.wait_ge(lut_pool, len(POOL_LOOKUPS))
                    for name, read in (("gate", gu_gate), ("up", gu_hid)):
                        dst = bank(read, FT * b + u + 1)
                        w = wffn[name]
                        split_product(dst[0:rows, :],
                                      [(lambda a, c=c: w[:, a, c, u * P:u * P + rows],
                                        lambda m, c=c: hT[1][:, m, c, :]) for c in range(NC)], gu_mm,
                                      (h_lo[1], NC * b + 1))
                elif kind == "dn":
                    dst = gen[begun(kind, u, turn[0])] if v == 2 else bank(dn_gate, NT * b + u + 1)
                    for f in {0: range(FT), 1: range(FT - 1), 2: range(FT - 1, FT)}[v]:
                        pe.wait_ge(hid_lo, FT * b + f + 1)
                        rows = P if f < FT - 1 else LAST_F
                        for k, (a, m) in enumerate(((0, 0), (0, 1), (1, 0))):
                            mm = pe.matmul(dst[:, 0:HID], hidT[0:rows, a, f, u * P:(u + 1) * P],
                                           wffn["down"][0:rows, m, f, :], start=(f == 0 and k == 0),
                                           stop=(f == FT - 1 and k == 2))
                    if v != 1:
                        mm.then_inc(dn_mm, 1)

            pe.wait_ge(ident_set, 1)
            for kind, db, u, v in PROLOGUE:
                filler(kind, db, u, v)

            def attend(b, s, n, first):
                new, old = to_transpose(b, s, n, first), to_multiply(b, s, n, first)
                if new:
                    transposes(*new)
                if old:
                    values(*old)

            def project(b, s, n, first):
                old = to_project(b, s, n, first)
                if old:
                    out_projection(*old)

            per_batch = {sc_max: NR * STEPS, v_lo: 2 * NT, o_add: STEPS, q_lo: NR * NG, k_lo: NG}
            start = []

            def slots(b, first, last):
                if not first:
                    if not entry:
                        entry.extend(users)
                        start.append(turn[0])
                    assert all(u is v for (u, _), (v, _) in zip(users, entry)) and (turn[0] - start[0]) % RING == 0
                    users[:] = [(u, n + per_batch[u] * (b - 1)) for u, n in entry]
                fill = fillers(first, last)
                for s in range(STEPS):
                    for n in range(NR):
                        scores(b, s, n)
                        attend(b, s, n, first)
                        for kind, db, u, v in share(fill[s], n):
                            filler(kind, b + db, u, v)
                        project(b, s, n, first)

            def tail():
                for s in range(STEPS, STEPS + LAG_O):
                    for n in range(NR):
                        attend(NB - 1, s, n, False)
                        project(NB - 1, s, n, False)
                for kind, _, u, v in TAIL:
                    filler(kind, NB - 1, u, v)

            batches(pe, slots, tail)

        @block.scalar
        def _(act):
            def high(dst, src, ready, count, done, scale=1.0):
                act.wait_ge(ready, count)
                act.activation(dst, src, ACT.Copy, scale=scale).then_inc(done, 1)

            def split_weight(n):
                kind, g = CHUNKS[n]
                dst = chunk_view(kind, g, 0)
                act.wait_ge(*chunk_at(n)[1:])
                act.activation(dst, chunk_stage(kind, n), ACT.Copy, scale=SC).then_inc(w_hi, 1)

            def lookup(op, n):
                kind, t, c0, cn, rows = PIECES[n]
                if op == "high":
                    act.wait_ge(lut_dve, done(DVE_LOOKUPS, "choose04", n))
                    act.activation(wffn[kind][0:rows, 0, t, c0:c0 + cn], slot_of[0][n % 2][0:rows, 0:cn],
                                   ACT.Copy).then_inc(lut_act, 1)
                    return
                freed = {"pair3": "choose02", "pair6": "choose46", "pair7": "choose67",
                         "bit3": "choose04"}
                if n:
                    act.wait_ge(lut_dve, done(DVE_LOOKUPS, freed[op], n - 1))
                if op == "bit3":
                    act.activation(bits[3][0][0:rows, 0:cn], idx[0:rows, n % 2, 0:cn], ACT.Relu,
                                   bias=minus_7[0:rows, :]).then_inc(lut_act, 1)
                    return
                k = int(op[-1])
                act.wait_ge(lut_dve, done(DVE_LOOKUPS, "bit0", n))
                act.activation(slot_of[k][n % 2][0:rows, 0:cn], bits[0][n % 2][0:rows, 0:cn], ACT.Identity,
                               bias=lutb[0:rows, 2 * k:2 * k + 1], scale=lutd[0:rows, k:k + 1]).then_inc(lut_act, 1)

            def normalise(which, b, i, count):
                act.wait_ge(ln_nmr[which], count)
                src = xn[0] if which == 0 else x1
                act.activation(xn[which][:, i, :], src[:, i, :], ACT.Identity, bias=nmr[:, which, i:i + 1],
                               scale=rstd[:, which, i:i + 1]).then_inc(ln_xn[which], 1)

            def filler(kind, b, u, v, turn):
                if kind in ("h1", "h2"):
                    if v == 1:
                        return
                    if v == 2:
                        turn = begun(kind, u, turn)
                    which = int(kind == "h2")
                    act.wait_ge(h_mm[which], NC * b + u + 1)
                    if u == 0 and isinstance(b, int) and b == 0 or which == 1:
                        act.wait_ge(mod_out, 2 * which + 2)
                    if which == 1:
                        act.wait_ge(row_out, NB)
                    act.activation(hf[:, which, u, :], gen[turn][:, :], ACT.Identity,
                                   bias=modT[:, 2 * which, u, bass.ds(b, 1)],
                                   scale=modT[:, 2 * which + 1, u, bass.ds(b, 1)]).then_inc(h_f[which], 1)
                    act.wait_ge(h_f[which], NC * b + u + 1)
                    act.activation(hT[which][:, 0, u, :], hf[:, which, u, :], ACT.Copy).then_inc(h_hi[which], 1)
                elif kind == "q":
                    high(qT[:, u % 2, 0, v, :], gen[turn][:, :], q_mm, NR * (NG * b + u) + v + 1, q_hi, 1 / SC)
                elif kind == "k":
                    high(kT[:, u % 2, 0, :], gen[turn][:, :], k_mm, NG * b + u + 1, k_hi, 1 / SC)
                elif kind == "v":
                    high(vS[:, u, 0, v, :], gen[turn][:, 0:2 * HD], v_mm, 2 * NT * b + NT * u + v + 1, v_hi, 1 / SC)
                elif kind == "gu":
                    rows = P if u < FT - 1 else LAST_F
                    n = FT * b + u
                    act.wait_ge(gu_mm, 2 * n + 2)
                    if u >= 2:
                        act.wait_ge(hid_lo, n - 1)
                    act.activation(act_t[0:rows, u % 2, :], gen[turn][0:rows, :], ACT.Tanh,
                                   scale=0.5 / SC).then_inc(gu_tanh, 1)
                elif kind == "hh":
                    rows = P if u < FT - 1 else LAST_F
                    high(hidT[0:rows, 0, u, :], act_t[0:rows, u % 2, :], gu_hid, FT * b + u + 1, hid_hi)

            act.wait_ge(minus_7_set, 1)
            act.wait_ge(c_in, 16)
            act.activation(cth[:, :, :], cin[:, :, :], ACT.Tanh, scale=0.5).then_inc(c_tanh, 1)
            split_weight(0)
            for i in range(NT):
                normalise(0, 0, i, 1)
            split_weight(1)
            turn = [0]
            for kind, db, u, v in PROLOGUE:
                if kind == "k":
                    for n in range(2, CHUNKS_EARLY):
                        split_weight(n)
                filler(kind, db, u, v, turn[0] % RING)
                turn[0] += banks_of(kind, v)

            def high_probs(b, s, j):
                kt = key_tile(b, s, j)
                ring = in_batch(s, j) % PTRING
                if not (isinstance(b, int) and kt < PTRING):
                    act.wait_ge(pv_mm, kt - PTRING + 1)
                high(pT[:, ring, 0, :], pt_ps[ring % 2][:, :], pt_mm, kt + 1, pt_hi, SC)

            def exponent(b, s, n):
                head = NR * (STEPS * b + s) + n
                keys = (TILE_OF[s % NT] + 1) * P
                act.wait_ge(sc_max, head + 1)
                p = prob[:, s % PRING, n, 0:keys]
                act.activation(p, p, ACT.Exp, bias=nmax[:, s % PRING, n:n + 1], scale=-1.0,
                               accum_out=rsum[:, s % PRING, n:n + 1]).then_inc(sc_exp, 1)

            def high_out(b, s):
                step = STEPS * b + s
                if not (isinstance(b, int) and step < 2):
                    act.wait_ge(o_mm, step - 1)
                high(oT[:, s % 2, 0, :, :], ot_ps[s % 2][:, :].rearrange("p (h n) -> p h n", h=NR),
                     pv_mm, key_tile(b, s, TILE_OF[s % NT]) + 1, ot_hi, 1 / SC)

            def attend(b, s, n, first):
                done, new = to_collect(b, s, n, first), to_transpose(b, s, n, first)
                if done:
                    high_out(*done)
                if new:
                    high_probs(*new)

            def slots(b, first, last):
                fill = fillers(first, last)
                for s in range(STEPS):
                    if first:
                        for n in CHUNK_SLOTS.get(s, []):
                            split_weight(n)
                    for n in range(NR):
                        attend(b, s, n, first)
                        if first:
                            for _, op, m in lookups(ACT_LOOKUPS, s, n):
                                lookup(op, m)
                        turn[0] += 1
                        if s == LN2_SLOT + 1 and not first:
                            normalise(1, b - 1, n, b)
                        if s == LN1_SLOT + 1 and not last:
                            normalise(0, b + 1, n, b + 2)
                        for kind, db, u, v in share(fill[s], n):
                            filler(kind, b + db, u, v, turn[0] % RING)
                            turn[0] += banks_of(kind, v)
                        exponent(b, s, n)
                        turn[0] += to_project(b, s, n, first) is not None

            def tail():
                for s in range(STEPS, STEPS + LAG_O):
                    for n in range(NR):
                        attend(NB - 1, s, n, False)
                        old = to_project(NB - 1, s, n, False)
                        if old:
                            turn[0] += 1
                            r = old[1] % NT
                            if r:
                                normalise(1, NB - 1, TILE_OF[r - 1], NB + r - 1)
                normalise(1, NB - 1, TILE_OF[NT - 1], NB + NT - 1)
                for kind, _, u, v in TAIL:
                    filler(kind, NB - 1, u, v, turn[0] % RING)
                    turn[0] += banks_of(kind, v)

            batches(act, slots, tail)

        @block.vector
        def _(dve):
            def hold():
                dve.nop(nofuse=True)

            def low(dst, src, hi, ready, count, done, scale):
                dve.wait_ge(ready, count)
                dve.scalar_tensor_tensor(out=dst, in0=src, scalar=scale, in1=hi,
                                         op0=ALU.mult, op1=ALU.subtract).then_inc(done, 1)

            def split_weight(n):
                kind, g = CHUNKS[n]
                low(chunk_view(kind, g, 1), chunk_stage(kind, n), chunk_view(kind, g, 0), w_hi, n + 1, w_lo, SC)

            def lookup(op, n):
                kind, t, c0, cn, rows = PIECES[n]
                if op.startswith("bit"):
                    k = int(op[-1])
                    if k == 0:
                        dve.wait_ge(idx_in[n % 2], 16 * (n // 2 + 1))
                        if n >= 2:
                            dve.wait_ge(lut_act, done(ACT_LOOKUPS, "pair7", n - 2))
                            dve.wait_ge(lut_pool, done(POOL_LOOKUPS, "pair5", n - 2))
                    elif n:
                        dve.wait_ge(lut_dve, done(DVE_LOOKUPS, {1: "choose67", 2: "choose46"}[k], n - 1))
                    dve.tensor_scalar(bits[k][n % 2][0:rows, 0:cn], idx[0:rows, n % 2, 0:cn], 1 << k, None,
                                      ALU.bitwise_and).then_inc(lut_dve, 1)
                    return
                x, y = int(op[-2]), int(op[-1])
                made = {"choose23": "pair3", "choose67": "pair7", "choose04": "bit3"}
                chosen = {"choose01": "bit1", "choose02": "choose23", "choose46": "choose67", "choose04": "choose46"}
                if op in made:
                    dve.wait_ge(lut_act, done(ACT_LOOKUPS, made[op], n))
                if op in ("choose01", "choose23", "choose45"):
                    dve.wait_ge(lut_pool, done(POOL_LOOKUPS, {1: "pair1", 3: "pair2", 5: "pair5"}[y], n))
                if op in chosen:
                    dve.wait_ge(lut_dve, done(DVE_LOOKUPS, chosen[op], n))
                dve.copy_predicated(slot_of[x][n % 2][0:rows, 0:cn], bits[MASK_BIT[op]][n % 2][0:rows, 0:cn],
                                    slot_of[y][n % 2][0:rows, 0:cn]).then_inc(lut_dve, 1)

            def statistics(which, b, i):
                src = xn[0] if which == 0 else x1
                if which == 0 and i == 0:
                    dve.wait_ge(x_in, 16 * (b + 1))
                dve.bn_stats(stats[:, which, i, :], src[:, i, :]).then_inc(ln_stat[which], 1)

            def aggregate(which, b, i, k):
                dve.wait_ge(ln_stat[which], NT * b + k + 1)
                hold()
                dve.bn_aggr(mv[:, which, i, :], stats[:, which, i, :]).then_inc(ln_mv[which], 1)

            def variance(which, count, i=slice(0, NT)):
                dve.wait_ge(ln_mv[which], count)
                dve.tensor_scalar(mv[:, which, i, 0], mv[:, which, i, 0], -1.0, None, ALU.mult)
                dve.tensor_scalar(mv[:, which, i, 1], mv[:, which, i, 1], EPS, None, ALU.add).then_inc(ln_eps[which], 1)

            def out_add(b, s, turn):
                g, i = s // NT, TILE_OF[s % NT]
                step = STEPS * b + s
                dve.wait_ge(o_mm, step + 1)
                if isinstance(b, int) and b == 0 and s == 0:
                    dve.wait_ge(bo_in, 16)
                if g:
                    dve.wait_ge(o_add, step - NT + 1)
                dve.scalar_tensor_tensor(out=acc[:, i, :], in0=gen[turn][:, 0:HID], scalar=1 / SC,
                                         in1=(acc[:, i, :] if g else bo_row[:, :]),
                                         op0=ALU.mult, op1=ALU.add).then_inc(o_add, 1)
                if g == NG - 1:
                    dve.wait_ge(o_add, step + 1)
                    dve.tensor_tensor(acc[:, i, :], acc[:, i, :], row(b, 0), ALU.mult).then_inc(x1_gate, 1)
                    dve.wait_ge(x1_gate, NT * b + s % NT + 1)
                    if s % NT == 0:
                        dve.wait_ge(x1_in, 16 * (b + 1))
                    dve.tensor_tensor(x1[:, i, :], x1[:, i, :], acc[:, i, :], ALU.add).then_inc(x1_sum, 1)
                    dve.wait_ge(x1_sum, NT * b + s % NT + 1)
                    statistics(1, b, i)
                    aggregate(1, b, i, s % NT)

            def row(b, which):
                return grow[:, bass.ds(b, 1), which, :].rearrange("p o n -> p (o n)")

            def filler(kind, b, u, v, turn):
                if kind in ("h1", "h2") and v >= 2:
                    which = int(kind == "h2")
                    low(hT[which][:, 1, u, :], hf[:, which, u, :], hT[which][:, 0, u, :],
                        h_hi[which], NC * b + u + 1, h_lo[which], 1.0)
                elif kind == "q":
                    low(qT[:, u % 2, 1, v, :], gen[turn][:, :], qT[:, u % 2, 0, v, :],
                        q_hi, NR * (NG * b + u) + v + 1, q_lo, 1 / SC)
                elif kind == "k":
                    low(kT[:, u % 2, 1, :], gen[turn][:, :], kT[:, u % 2, 0, :], k_hi, NG * b + u + 1, k_lo, 1 / SC)
                elif kind == "v":
                    low(vS[:, u, 1, v, :], gen[turn][:, 0:2 * HD], vS[:, u, 0, v, :],
                        v_hi, 2 * NT * b + NT * u + v + 1, v_lo, 1 / SC)
                elif kind == "mod":
                    dve.wait_ge(mod_mm, u + 1)
                    md = gen[turn][:, 0:2 * NC * NB].rearrange("p (m n) -> p m n", m=2)
                    mt = modT[:, 2 * u:2 * u + 2, :, :].rearrange("p m c b -> p m (c b)")
                    dve.tensor_copy(mt[:, 0, :], md[:, 0, :]).then_inc(mod_out, 1)
                    dve.tensor_scalar(mt[:, 1, :], md[:, 1, :], 1.0, None, ALU.add).then_inc(mod_out, 1)
                elif kind == "row":
                    dve.wait_ge(row_mm, u + 1)
                    sgn, mag = hf[:, 1, 0, :], hf[:, 1, 1, :]
                    dve.tensor_scalar(sgn, gen[turn][:, :], 0.0, 2.0, ALU.is_ge, ALU.mult).then_inc(row_sgn, 1)
                    dve.wait_ge(row_sgn, 4 * u + 1)
                    dve.scalar_tensor_tensor(out=mag, in0=sgn, scalar=-1.0, in1=gen[turn][:, :],
                                             op0=ALU.add, op1=ALU.mult).then_inc(row_sgn, 1)
                    dve.wait_ge(row_sgn, 4 * u + 2)
                    dve.tensor_scalar(mag, mag, GUARD, None, ALU.max).then_inc(row_sgn, 1)
                    dve.wait_ge(row_sgn, 4 * u + 3)
                    dve.scalar_tensor_tensor(out=grow[:, u, :, :].rearrange("p a n -> p (a n)"), in0=sgn, scalar=-1.0,
                                             in1=mag, op0=ALU.add, op1=ALU.mult).then_inc(row_sgn, 1)
                    dve.wait_ge(row_sgn, 4 * u + 4)
                    dve.tensor_scalar(grow[:, u, 1, :], grow[:, u, 1, :], 1 / SC, None, ALU.mult).then_inc(row_out, 1)
                elif kind == "gu":
                    rows = P if u < FT - 1 else LAST_F
                    n = FT * b + u
                    t = act_t[0:rows, u % 2, :]
                    dve.wait_ge(gu_tanh, n + 1)
                    dve.scalar_tensor_tensor(out=t, in0=t, scalar=1.0, in1=gen[turn][0:rows, :],
                                             op0=ALU.add, op1=ALU.mult).then_inc(gu_gate, 1)
                    dve.wait_ge(gu_gate, n + 1)
                    dve.scalar_tensor_tensor(out=t, in0=t, scalar=0.5 / (SC * SC), in1=gen[(turn + 1) % RING][0:rows, :],
                                             op0=ALU.mult, op1=ALU.mult).then_inc(gu_hid, 1)
                elif kind == "dn" and v != 1:
                    n = NT * b + u
                    if v == 2:
                        turn = begun(kind, u, turn)
                    dve.wait_ge(dn_mm, n + 1)
                    if u >= 2:
                        dve.wait_ge(out_sent[u % 2], 32 * b + 16 * (u // 2))
                    dve.tensor_tensor(outb[:, u % 2, :], gen[turn][:, 0:HID], row(b, 1), ALU.mult).then_inc(dn_gate, 1)
                    dve.wait_ge(dn_gate, n + 1)
                    dve.tensor_tensor(outb[:, u % 2, :], outb[:, u % 2, :], x1[:, u, :], ALU.add).then_inc(dn_out, 1)

            dve.wait_ge(c_tanh, 1)
            dve.scalar_tensor_tensor(out=cth[:, :, :], in0=cth[:, :, :], scalar=1.0, in1=cin[:, :, :],
                                     op0=ALU.add, op1=ALU.mult).then_inc(c_twice, 1)
            dve.wait_ge(c_twice, 1)
            dve.tensor_scalar(csl[:, :, :], cth[:, :, :], 0.5, None, ALU.mult).then_inc(c_silu, 1)
            dve.wait_ge(c_silu, 1)
            for i in range(NT):
                statistics(0, 0, i)
            for i in range(NT):
                aggregate(0, 0, i, i)
            variance(0, NT)
            split_weight(0)
            turn = [0]

            def prepare():
                pairs = lutb[:, :].rearrange("p (k two) -> p k two", two=2)
                dve.wait_ge(lut_in, 16)
                dve.tensor_scalar(lutb[:, :], lutb[:, :], SC, None, ALU.mult).then_inc(lut_table, 1)
                dve.tensor_copy(crep[:, :, :, :],
                                csl[:, :, :].unsqueeze(3).broadcast_to([P, NC, NB, P])).then_inc(c_rep, 1)
                dve.wait_ge(lut_table, 1)
                dve.tensor_tensor(lutd[:, :], pairs[:, :, 1], pairs[:, :, 0], ALU.subtract).then_inc(lut_table, 1)
                dve.wait_ge(lut_table, 2)

            for kind, db, u, v in PROLOGUE:
                if kind == "k":
                    for n in range(2, CHUNKS_EARLY):
                        split_weight(n)
                    prepare()
                filler(kind, db, u, v, turn[0] % RING)
                turn[0] += banks_of(kind, v)
                if kind == "mod":
                    split_weight(1)

            def low_probs(b, s, j):
                ring = in_batch(s, j) % PTRING
                low(pT[:, ring, 1, :], pt_ps[ring % 2][:, :], pT[:, ring, 0, :], pt_hi, key_tile(b, s, j) + 1, pt_lo, SC)

            def maximum(b, s, n, first, turn):
                head = NR * (STEPS * b + s) + n
                keys = (TILE_OF[s % NT] + 1) * P
                dve.wait_ge(sc_mm, head + 1)
                if n == 0 and (s >= PRING or not first):
                    ob, os_ = (b, s - PRING) if s >= PRING else (b - 1, s - PRING + STEPS)
                    dve.wait_ge(pt_mm, key_tile(ob, os_, TILE_OF[os_ % NT]) + 1)
                if first and s == 0 and n == 0:
                    dve.wait_ge(mask_set, 1)
                if first and s == 2 and n == 0:
                    dve.wait_ge(row_mm, NB)
                hold()
                dve.tensor_tensor_reduce(out=prob[:, s % PRING, n, 0:keys], in0=gen[turn][:, 0:keys],
                                         in1=mask[:, S - keys:S], scale=-1.0, scalar=-NEG, op0=ALU.add, op1=ALU.min,
                                         accum_out=nmax[:, s % PRING, n:n + 1]).then_inc(sc_max, 1)

            def inverse(b, s):
                step = STEPS * b + s
                dve.wait_ge(sc_exp, NR * (step + 1))
                if not (isinstance(b, int) and step < PRING):
                    dve.wait_ge(p_norm, step - PRING + 1)
                dve.reciprocal(rinv[:, s % PRING, :], rsum[:, s % PRING, :]).then_inc(p_inv, 1)

            def low_out(b, s):
                low(oT[:, s % 2, 1, :, :], ot_ps[s % 2][:, :].rearrange("p (h n) -> p h n", h=NR), oT[:, s % 2, 0, :, :],
                    ot_hi, STEPS * b + s + 1, ot_lo, 1 / SC)

            def attend(b, s, n, first):
                done, new = to_collect(b, s, n, first), to_transpose(b, s, n, first)
                if done:
                    low_out(*done)
                if new:
                    low_probs(*new)

            def project(b, s, n, first):
                old = to_project(b, s, n, first)
                if old:
                    out_add(*old, turn[0] % RING)
                    turn[0] += 1

            def slots(b, first, last):
                fill = fillers(first, last)
                for s in range(STEPS):
                    for n in range(NR):
                        maximum(b, s, n, first, turn[0] % RING)
                        turn[0] += 1
                        if n == 0 and not (first and s == 0):
                            inverse(*((b, s - 1) if s else (b - 1, STEPS - 1)))
                        attend(b, s, n, first)
                        if first:
                            for m in CHUNK_SLOTS.get(s, []) if n == 0 else []:
                                split_weight(m)
                            for _, op, m in lookups(DVE_LOOKUPS, s, n):
                                lookup(op, m)
                        for kind, db, u, v in share(fill[s], n):
                            filler(kind, b + db, u, v, turn[0] % RING)
                            turn[0] += banks_of(kind, v)
                        project(b, s, n, first)
                    if s == LN2_SLOT and not first:
                        variance(1, NT * b)
                    if LN1_SLOT - NT <= s < LN1_SLOT and not last:
                        i = s - LN1_SLOT + NT
                        statistics(0, b + 1, i)
                        aggregate(0, b + 1, i, i)
                    if s == LN1_SLOT and not last:
                        variance(0, NT * (b + 2))

            def tail():
                inverse(NB - 1, STEPS - 1)
                for s in range(STEPS, STEPS + LAG_O):
                    for n in range(NR):
                        attend(NB - 1, s, n, False)
                        project(NB - 1, s, n, False)
                        old = to_project(NB - 1, s, n, False)
                        if old:
                            r = old[1] % NT
                            variance(1, NT * (NB - 1) + r + 1, slice(TILE_OF[r], TILE_OF[r] + 1))
                for kind, _, u, v in TAIL:
                    filler(kind, NB - 1, u, v, turn[0] % RING)
                    turn[0] += banks_of(kind, v)

            batches(dve, slots, tail)

        @block.gpsimd
        def _(pool):
            pool.memset(ident[:, :], 0.0).then_inc(ident_0, 1)
            pool.wait_ge(ident_0, 1)
            pool.affine_select(out=ident[:, :], in_=ident[:, :], compare_op=ALU.not_equal, fill=1.0, base=0,
                               pattern=[[-1, P]], channel_multiplier=1).then_inc(ident_set, 1)
            pool.memset(minus_7[:, :], -7.0).then_inc(minus_7_set, 1)
            pool.memset(mhalf[:, :], -0.5).then_inc(half_set, 1)
            pool.wait_ge(half_set, 1)

            def root(which, b, count, i=slice(0, NT)):
                pool.wait_ge(ln_eps[which], count)
                if not (isinstance(b, int) and b == 0):
                    pool.wait_ge(ln_xn[which], NT * b)
                pool.tensor_tensor(rstd[:, which, i], mv[:, which, i, 1], mhalf[:, i], ALU.pow).then_inc(ln_rstd[which], 1)
                pool.wait_ge(ln_rstd[which], count)
                pool.tensor_tensor(nmr[:, which, i], mv[:, which, i, 0], rstd[:, which, i], ALU.mult).then_inc(ln_nmr[which], 1)

            def filler(kind, b, u, v):
                if kind in ("h1", "h2") and v == 0:
                    which = int(kind == "h2")
                    pool.wait_ge(h_hi[which], NC * b + u + 1)
                    pool.tensor_tensor(hT[which][:, 1, u, :], hf[:, which, u, :], hT[which][:, 0, u, :],
                                       ALU.subtract).then_inc(h_lo[which], 1)
                elif kind == "hh":
                    rows = P if u < FT - 1 else LAST_F
                    pool.wait_ge(hid_hi, FT * b + u + 1)
                    pool.tensor_tensor(hidT[0:rows, 1, u, :], act_t[0:rows, u % 2, :], hidT[0:rows, 0, u, :],
                                       ALU.subtract).then_inc(hid_lo, 1)

            def divide(b, s):
                keys = (TILE_OF[s % NT] + 1) * P
                pool.wait_ge(p_inv, STEPS * b + s + 1)
                p = prob[:, s % PRING, :, 0:keys]
                pool.tensor_tensor(p, p, rinv[:, s % PRING, :].unsqueeze(2).broadcast_to([P, NR, keys]),
                                   ALU.mult).then_inc(p_norm, 1)

            def lookup(op, n):
                kind, t, c0, cn, rows = PIECES[n]
                if op == "low":
                    pool.wait_ge(lut_act, done(ACT_LOOKUPS, "high", n))
                    w = wffn[kind]
                    pool.tensor_tensor(w[0:rows, 1, t, c0:c0 + cn], slot_of[0][n % 2][0:rows, 0:cn],
                                       w[0:rows, 0, t, c0:c0 + cn], ALU.subtract).then_inc(lut_pool, 1)
                    return
                k = int(op[-1])
                pool.wait_ge(lut_dve, done(DVE_LOOKUPS, "bit0", n))
                if k in (1, 2, 5) and n:
                    pool.wait_ge(lut_dve, done(DVE_LOOKUPS, {1: "choose01", 2: "choose02", 5: "choose45"}[k], n - 1))
                elif k == 4 and n >= 2:
                    pool.wait_ge(lut_dve, done(DVE_LOOKUPS, "choose04", n - 2))
                elif k == 0 and n >= 2:
                    pool.wait_ge(lut_pool, done(POOL_LOOKUPS, "low", n - 2))
                pool.tensor_scalar(slot_of[k][n % 2][0:rows, 0:cn], bits[0][n % 2][0:rows, 0:cn],
                                   lutd[0:rows, k:k + 1], lutb[0:rows, 2 * k:2 * k + 1],
                                   ALU.mult, ALU.add).then_inc(lut_pool, 1)

            root(0, 0, 1)
            pool.memset(mask[:, :], 0.0).then_inc(mask_0, 1)
            pool.wait_ge(mask_0, 1)
            pool.affine_select(out=mask[:, S - P:S], in_=mask[:, S - P:S], compare_op=ALU.is_ge, fill=NEG, base=0,
                               pattern=[[-1, P]], channel_multiplier=1).then_inc(mask_set, 1)
            for kind, db, u, v in PROLOGUE:
                filler(kind, db, u, v)

            def slots(b, first, last):
                fill = fillers(first, last)
                for s in range(STEPS):
                    if not (first and s == 0):
                        divide(*((b, s - 1) if s else (b - 1, STEPS - 1)))
                    for n in range(NR):
                        for kind, db, u, v in share(fill[s], n):
                            filler(kind, b + db, u, v)
                        if first:
                            for _, op, m in lookups(POOL_LOOKUPS, s, n):
                                lookup(op, m)
                    if s == LN2_SLOT and not first:
                        root(1, b - 1, b)
                    if s == LN1_SLOT and not last:
                        root(0, b + 1, b + 2)

            def tail():
                divide(NB - 1, STEPS - 1)
                for r in range(NT):
                    root(1, NB - 1, NB + r, slice(TILE_OF[r], TILE_OF[r] + 1))
                for kind, _, u, v in TAIL:
                    filler(kind, NB - 1, u, v)

            batches(pool, slots, tail)


_INS = [("x", "L0_attn_hidden_states"), ("wqT", "L0_attn_Wq"), ("wkT", "L0_attn_Wk"), ("wvT", "L0_attn_Wv"),
        ("woT", "L0_attn_Wo"), ("bo", "L0_attn_bo"), ("lut", "L0_ffn_lut"), ("gate_iT", "L0_ffn_gate_idx"),
        ("up_iT", "L0_ffn_up_idx"), ("down_iT", "L0_ffn_down_idx"), ("cT", "L0_c"), ("wmod", "L0_wmod")]


def kernel(**inputs):
    import numpy as np
    import concourse.bacc as bacc
    from concourse.bass_utils import run_bass_kernel_spmd as run

    nc = bacc.Bacc("TRN2", target_bir_lowering=False, num_devices=1)
    arrays, args = {}, []
    for short, name in _INS:
        a = np.asarray(inputs[name])
        a = np.ascontiguousarray(a.T if short.endswith("T") else a)
        arrays[short] = a
        args.append(nc.dram_tensor(short, a.shape, mybir.dt.from_np(a.dtype), kind="ExternalInput").ap())
    args.append(nc.dram_tensor("y", (NB, S, HID), F32, kind="ExternalOutput").ap())
    block_program(nc, *args)
    return run(nc, [arrays], core_ids=[0]).results[0]["y"]
```
